# Optimizing a Trainium2 kernel written in Bass

```python
import numpy as np
import jax
import jax.numpy as jnp

def _softmax(x, axis=-1):
    return jax.nn.softmax(x, axis=axis)

def _gelu(x):
    return jax.nn.gelu(x, approximate=True)

def _silu(x):
    return jax.nn.silu(x)

def _sigmoid(x):
    return jax.nn.sigmoid(x)

def _layernorm(x, axis=-1, eps=1e-05):
    m = jnp.mean(x, axis=axis, keepdims=True)
    v = jnp.var(x, axis=axis, keepdims=True)
    return (x - m) / jnp.sqrt(v + eps)

def _scatter_add(tgt, idx, src, axis=0):
    return tgt.at[idx].add(src)

def _segment_sum(src, seg, n):
    return jax.ops.segment_sum(src, seg, n)
kernel_name = 'mk_adaln_d1_jaxref_r8_23b041'

def setup_inputs(seed: int=0):
    np.random.seed(seed)
    _w = jnp.asarray

    def _L0_attn_setup():
        import jax, jax.numpy as jnp
        import numpy as np
        DIM = 128
        HEADS = 16
        DIM_HEAD = DIM // HEADS
        B, N = (4, 128)
        key = jax.random.key(seed)
        ks = jax.random.split(key, 8)
        s = 1.0 / np.sqrt(DIM)
        inp = {'x': jax.random.normal(ks[0], (B, N, DIM), dtype=jnp.float32), 'Wq': jax.random.normal(ks[1], (DIM, DIM), dtype=jnp.float32) * s, 'Wk': jax.random.normal(ks[2], (DIM, DIM), dtype=jnp.float32) * s, 'Wv': jax.random.normal(ks[3], (DIM, DIM), dtype=jnp.float32) * s, 'Wproj': jax.random.normal(ks[4], (DIM, DIM), dtype=jnp.float32) * s, 'bproj': jnp.zeros((DIM,), dtype=jnp.float32), 'Wpre': jax.random.normal(ks[5], (DIM, DIM), dtype=jnp.float32) * s, 'bpre': jnp.zeros((DIM,), dtype=jnp.float32), 'pi': jnp.full((1,), 0.5, dtype=jnp.float32)}
        return inp
    _L0_attn_in = _L0_attn_setup()

    def _L0_ffn_setup():
        import jax, jax.numpy as jnp
        import numpy as np
        B, S, H = (2, 256, 128)
        N, F, SF, K = (16, 128, 512, 1)
        key = jax.random.key(seed)
        ks = jax.random.split(key, 7)
        std = 0.02
        return {'hidden_states': jax.random.normal(ks[0], (B, S, H), dtype=jnp.float32), 'router_w': jax.random.normal(ks[1], (N, H), dtype=jnp.float32) * std, 'gate_up_proj': jax.random.normal(ks[2], (N, H, 2 * F), dtype=jnp.float32) * std, 'down_proj': jax.random.normal(ks[3], (N, F, H), dtype=jnp.float32) * std, 'shared_gate_w': jax.random.normal(ks[4], (SF, H), dtype=jnp.float32) * std, 'shared_up_w': jax.random.normal(ks[5], (SF, H), dtype=jnp.float32) * std, 'shared_down_w': jax.random.normal(ks[6], (H, SF), dtype=jnp.float32) * std}
    _L0_ffn_in = _L0_ffn_setup()
    _L0_c = _w((lambda *s: np.random.randn(*s).astype(np.float32) * 0.05)(2, 128))
    _L0_wmod = _w((lambda *s: np.random.randn(*s).astype(np.float32) * 0.05)(128, 6 * 128) * 128 ** (-0.5))
    _d = {'L0_attn_x': _L0_attn_in['x'], 'L0_attn_Wq': _L0_attn_in['Wq'], 'L0_attn_Wk': _L0_attn_in['Wk'], 'L0_attn_Wv': _L0_attn_in['Wv'], 'L0_attn_Wproj': _L0_attn_in['Wproj'], 'L0_attn_bproj': _L0_attn_in['bproj'], 'L0_attn_Wpre': _L0_attn_in['Wpre'], 'L0_attn_bpre': _L0_attn_in['bpre'], 'L0_attn_pi': _L0_attn_in['pi'], 'L0_ffn_router_w': _L0_ffn_in['router_w'], 'L0_ffn_gate_up_proj': _L0_ffn_in['gate_up_proj'], 'L0_ffn_down_proj': _L0_ffn_in['down_proj'], 'L0_ffn_shared_gate_w': _L0_ffn_in['shared_gate_w'], 'L0_ffn_shared_up_w': _L0_ffn_in['shared_up_w'], 'L0_ffn_shared_down_w': _L0_ffn_in['shared_down_w'], 'L0_c': _L0_c, 'L0_wmod': _L0_wmod}
    _x0 = _d['L0_attn_x']
    _d['L0_attn_x'] = jax.random.normal(jax.random.fold_in(jax.random.key(seed), 1), (2, 1024, 128), dtype=_x0.dtype)
    del _x0
    return _d

def reference(L0_attn_x, L0_attn_Wq, L0_attn_Wk, L0_attn_Wv, L0_attn_Wproj, L0_attn_bproj, L0_attn_Wpre, L0_attn_bpre, L0_attn_pi, L0_ffn_router_w, L0_ffn_gate_up_proj, L0_ffn_down_proj, L0_ffn_shared_gate_w, L0_ffn_shared_up_w, L0_ffn_shared_down_w, L0_c, L0_wmod):

    def _L0_attn_ref(x, Wq, Wk, Wv, Wproj, bproj, Wpre, bpre, pi):
        import jax, jax.numpy as jnp
        import numpy as np
        DIM = 128
        HEADS = 16
        DIM_HEAD = DIM // HEADS
        B, N = (4, 128)
        b, n, c = x.shape
        h, dh = (HEADS, DIM_HEAD)
        residual = x
        pre = jax.nn.silu(x @ Wpre + bpre)
        logits = jnp.einsum('bnc,bmc->bnm', pre, pre) / jnp.sqrt(jnp.float32(c))
        q = (x @ Wq).reshape(b, n, h, dh).transpose(0, 2, 1, 3)
        k = (x @ Wk).reshape(b, n, h, dh).transpose(0, 2, 1, 3)
        v = (x @ Wv).reshape(b, n, h, dh).transpose(0, 2, 1, 3)
        score = jnp.einsum('bhnd,bhmd->bhnm', q, k) / jnp.sqrt(jnp.float32(dh))
        final_logits = pi[0] * logits[:, None, :, :] + score
        attn = jax.nn.softmax(final_logits, axis=-1)
        out = jnp.einsum('bhnm,bhmd->bhnd', attn, v)
        out = out.transpose(0, 2, 1, 3).reshape(b, n, h * dh)
        out = out @ Wproj + bproj
        return out + residual

    def _L0_ffn_ref(hidden_states, router_w, gate_up_proj, down_proj, shared_gate_w, shared_up_w, shared_down_w):
        import jax, jax.numpy as jnp
        import numpy as np
        B, S, H = (2, 256, 128)
        N, F, SF, K = (16, 128, 512, 1)
        b, s, h = hidden_states.shape
        hidden = hidden_states.reshape(-1, h)
        t = hidden.shape[0]
        logits = hidden @ router_w.T
        top_vals, top_idx = jax.lax.top_k(logits, K)
        scores = jnp.full_like(logits, -jnp.inf)
        scores = scores.at[jnp.arange(t)[:, None], top_idx].set(top_vals)
        scores = jax.nn.sigmoid(scores.astype(jnp.float32)).astype(hidden.dtype)
        routed_in = hidden[None, :, :] * scores.T[:, :, None]
        gate_up = jnp.einsum('nth,nhf->ntf', routed_in, gate_up_proj)
        gate, up = jnp.split(gate_up, 2, axis=-1)
        routed_out = jnp.einsum('ntf,nfh->nth', up * jax.nn.silu(gate), down_proj)
        expert_sum = routed_out.sum(axis=0)
        shared = jax.nn.silu(hidden @ shared_gate_w.T) * (hidden @ shared_up_w.T) @ shared_down_w.T
        return (shared + expert_sum).reshape(b, s, h)
    x = L0_attn_x
    mod = (_silu(L0_c) @ L0_wmod).reshape(L0_c.shape[0], 6, 1, -1)
    sa, ca, ga, sb, cb, gb = (mod[:, 0], mod[:, 1], mod[:, 2], mod[:, 3], mod[:, 4], mod[:, 5])
    ga = (2 * (ga >= 0) - 1) * jnp.maximum(jnp.abs(ga), 0.25)
    gb = (2 * (gb >= 0) - 1) * jnp.maximum(jnp.abs(gb), 0.25)
    h = _layernorm(x, axis=-1) * (1 + ca) + sa
    x = x + ga * _L0_attn_ref(h, L0_attn_Wq, L0_attn_Wk, L0_attn_Wv, L0_attn_Wproj, L0_attn_bproj, L0_attn_Wpre, L0_attn_bpre, L0_attn_pi)
    h = _layernorm(x, axis=-1) * (1 + cb) + sb
    x = x + gb * _L0_ffn_ref(h, L0_ffn_router_w, L0_ffn_gate_up_proj, L0_ffn_down_proj, L0_ffn_shared_gate_w, L0_ffn_shared_up_w, L0_ffn_shared_down_w)
    return x

_drawn_inputs = setup_inputs


def setup_inputs(seed=0):
    import zlib

    import numpy as np

    out = dict(_drawn_inputs(seed))
    spreads = {'L0_attn_bproj': (0.0, 0.306), 'L0_attn_bpre': (0.0, 2.0)}
    factors = {'L0_attn_Wpre': 64.0,
     'L0_ffn_router_w': 8.0,
     'L0_ffn_gate_up_proj': 8.0,
     'L0_ffn_down_proj': 8.0,
     'L0_ffn_shared_gate_w': 8.0,
     'L0_ffn_shared_up_w': 8.0,
     'L0_ffn_shared_down_w': 8.0,
     'L0_attn_Wq': 8.0,
     'L0_attn_Wk': 8.0}
    for name, (base, spread) in spreads.items():
        noise = np.random.default_rng([zlib.crc32(name.encode()), seed]).standard_normal(out[name].shape)
        drawn = base * np.exp(spread * noise) if base else spread * noise
        out[name] = jnp.asarray(drawn.astype(out[name].dtype))
    for name, factor in factors.items():
        out[name] = (out[name] * factor).astype(out[name].dtype)
    return out
```

```python
from contextlib import ExitStack

import numpy as np

import concourse.bass as bass
from concourse import mybir

F32 = mybir.dt.float32
BF16 = mybir.dt.bfloat16
I32 = mybir.dt.int32
ALU = mybir.AluOpType
ACT = mybir.ActivationFunctionType
AX = mybir.AxisListType

P = 128
C = 128
HEADS = 16
DH = C // HEADS
BATCH = 2
SEQ = 1024
NT = SEQ // P
NTA = BATCH * NT
QB = 256
BLOCKS = BATCH * SEQ // QB
PAD = SEQ + QB
CH = 512
GH = 4
GROUPS = HEADS // GH
EPS = 1e-5
LOWEST = -3.0e38
Q_PART = (0, 1, 2, 0, 1, 0)
K_PART = (0, 0, 0, 1, 1, 2)
ROWS = 6 * DH
CROW = ROWS
PREV = 64
CHUNKS = HEADS * 4
STEPS = HEADS * 2
EXPERTS = 16
F = 128
SF = 512
MOE_TILES = NTA + EXPERTS
MOE_CHUNKS = MOE_TILES // 4
GRP = 4
NG = NTA // GRP
Q_RUNS = ((0, 3), (3, 2), (5, 1))
Q_DMAS = 2 * len(Q_RUNS) + 1
ONE_PAIR = float(np.array([0x3F803F80], np.uint32).view(np.float32)[0])
MINUS_ONE_PAIR = float(np.array([0xBF80BF80], np.uint32).view(np.float32)[0])


LOOPS = (BLOCKS - 2) // 2


def following(blk):
    t, b, i = blk
    return t + 1, 1 - b, i + b


def before(blk):
    t, b, i = blk
    return t - 1, 1 - b, i - (1 - b)


def build(nc, x, wq, wk, wv, wproj, bproj, wpre, bpre, pi, cond, wmod,
          router_w, gate_up_w, down_w, shared_gate_w, shared_up_w, shared_down_w, out):
    with ExitStack() as ctx:
        def sb(name, shape, dt=F32):
            return ctx.enter_context(nc.sbuf_tensor(name, shape, dt))

        def sem(name):
            return ctx.enter_context(nc.semaphore(name))

        q_dram = nc.dram_tensor("q_parts", [BATCH, 3 * DH, HEADS, PAD], BF16).ap()
        k_dram = nc.dram_tensor("k_parts", [BATCH, 3 * DH, HEADS, SEQ], BF16).ap()
        nk_dram = nc.dram_tensor("minus_k_parts", [BATCH, 3 * DH, HEADS, SEQ], BF16).ap()
        pre_dram = nc.dram_tensor("pre_scaled", [BATCH, P, PAD], F32).ap()
        sorted_dram = nc.dram_tensor("sorted_tokens", [MOE_TILES * P, C], F32).ap()
        expert_dram = nc.dram_tensor("expert_outputs", [MOE_TILES * P, C], F32).ap()
        h_dram = nc.dram_tensor("h_cols", [P, BATCH * SEQ], F32).ap()

        kd = sb("kd", [P, BATCH, HEADS, SEQ], BF16)
        qd = sb("qd", [P, 2, HEADS, QB], BF16)
        work = sb("work", [P, 2 * GH * NT * QB])
        probs = work[:, :].rearrange("p (s h m n) -> p s h m n", s=2, h=GH, m=NT)
        v_aug = sb("v_aug", [P, BATCH, NT, HEADS, DH + 1])
        preT = sb("preT", [P, BATCH, SEQ])
        pre_blk = sb("pre_blk", [P, 2, QB])
        logits = sb("logits", [P, 2, 2, SEQ])
        av_sb = sb("av_sb", [P, GROUPS, QB])
        attn = sb("attn", [P, BATCH, NT, C])
        junk = sb("junk", [P, 2, CH], BF16)
        row_max = sb("row_max", [P, 2, HEADS, 2, 2])
        neg_max = sb("neg_max", [P, 8, 2])
        c_parts = sb("c_parts", [P, 2, 2, 8], BF16)
        cT = sb("cT", [16, 2, QB], BF16)
        recip = sb("recip", [P, HEADS])
        ident = sb("ident", [P, P])
        ident_b = sb("ident_b", [P, P], BF16)
        zeros2 = sb("zeros2", [2, 8, QB], BF16)
        weights = sb("weights", [P, 5, C])
        mod_cols = sb("mod_cols", [P, 4, BATCH])
        gate_cols = sb("gate_cols", [P, 3, 2 * BATCH])
        mod_rows = sb("mod_rows", [P, BATCH, 4, C])
        small = sb("small", [P, 8])
        stats = sb("stats", [P, NTA, 6])
        mv = sb("mv", [P, NTA, 2])
        std = sb("std", [P, NTA])
        rstd = sb("rstd", [P, NTA])
        silu_in = sb("silu_in", [P, BATCH])
        silu_c = sb("silu_c", [P, BATCH])

        def view(at, n):
            return work[:, at:at + n]

        xs = view(0, 2048).rearrange("p (t c) -> p t c", t=NTA)
        xhat = view(2048, 2048).rearrange("p (t c) -> p t c", t=NTA)
        hT = view(4096, 2048).rearrange("p (b n) -> p b n", b=BATCH)
        qk32 = view(6144, 2048).rearrange("p (w n) -> p w n", w=2)
        rest = view(8192, 2048).rearrange("p (w n) -> p w n", w=2)
        wmod_sb = view(8192, 768)
        parts = view(10240, 4608).bitcast(BF16).rearrange("p (w s n) -> p w s n", w=3, s=3)
        preS = view(14848, 1024)
        gate_sign = view(14848, 512).rearrange("p (n c) -> p n c", n=4)
        gate_size = view(15360, 512).rearrange("p (n c) -> p n c", n=4)
        w_dh = view(16128, 256).rearrange("p (w n) -> p w n", w=2)
        gate_step = view(10240, 512).rearrange("p (n c) -> p n c", n=4)
        silu_cb = view(15872, 256).rearrange("p (b c) -> p b c", b=BATCH)

        kd32 = [kd[:, b, :, :].rearrange("p h n -> p (h n)").bitcast(F32) for b in range(BATCH)]
        w_gu = kd32[0][:, 0:4096]
        w_dn = kd32[0][:, 4096:6144]
        w_raw = kd32[0][:, 6144:7680].rearrange("p (w k c) -> p w k c", w=3, k=4)
        r_raw = kd32[0][0:EXPERTS, 7680:7808]
        x_back = logits[:, :, 0, :].rearrange("p b (t c) -> p b t c", c=C)
        h_back = logits[:, :, 1, :]
        w_gT = preT[:, 0, 0:SF]
        w_uT = preT[:, 0, SF:2 * SF]
        w_dT = preT[:, 1, 0:SF].rearrange("p (k c) -> p k c", k=4)
        w_rT = preT[:, 1, SF:SF + EXPERTS]
        aT = view(0, 1024).rearrange("p (u n) -> p u n", u=2)
        zT = view(1024, 1024).rearrange("p (u n) -> p u n", u=2)
        x1 = view(2048, 2048).rearrange("p (t c) -> p t c", t=NTA)
        h2 = view(4096, 2048).rearrange("p (t c) -> p t c", t=NTA)
        h2T = view(6144, 2048)
        acc = view(8192, 2048).rearrange("p (t c) -> p t c", t=NTA)
        ff_silu = view(10240, 1024).rearrange("p (u n) -> p u n", u=2)
        ff_act = view(11264, 1024).rearrange("p (u n) -> p u n", u=2)
        ff_out = view(12288, 1024).rearrange("p (u n) -> p u n", u=2)
        zpart = ff_silu
        ln_part = view(13312, 256).rearrange("p (u n) -> p u n", u=2)
        route = view(13568, 5 * 256).rearrange("p (k t e) -> p k t e", k=5, t=NTA)
        onehot_b = view(14848, 128).bitcast(BF16).rearrange("p (t e) -> p t e", t=NTA)
        upper_b = view(14976, 64).bitcast(BF16)
        ones_b = view(15040, 64).bitcast(BF16)
        tok = view(15104, 128).rearrange("p (k t) -> p k t", k=8)
        per_e = view(15232, 128).rearrange("p (k e) -> p k e", k=8)
        weight_e = view(15360, 16)
        upper32 = view(15376, 128)
        tab = work[0:1, 15504:15504 + MOE_TILES * EXPERTS].rearrange("p (j e) -> p j e", e=EXPERTS)
        tab_j = work[0:1, 16016:16016 + MOE_TILES]
        tab_jf = work[0:1, 16048:16048 + MOE_TILES]
        tab_e = work[0:1, 16080:16080 + MOE_TILES]
        rows = kd32[1][:, 0:2048].rearrange("p (t c) -> p t c", t=NTA)
        moe_x = kd32[1][:, 2048:3072].rearrange("p (u t c) -> p u t c", u=2, t=GRP)
        moe_xT = kd32[1][:, 3072:3584].rearrange("p (t n) -> p t n", t=GRP)
        moe_silu = kd32[1][:, 3584:4096].rearrange("p (t n) -> p t n", t=GRP)
        moe_act = kd32[1][:, 4096:4608].rearrange("p (t n) -> p t n", t=GRP)
        moe_aT = kd32[1][:, 4608:5120].rearrange("p (t n) -> p t n", t=GRP)
        moe_y = kd32[1][:, 5120:6144].rearrange("p (u t c) -> p u t c", u=2, t=GRP)
        got = kd32[1][:, 6144:8192].rearrange("p (t c) -> p t c", t=NTA)
        zero_rows = sb("zero_rows", [P, C])
        pos = sb("pos", [P, NTA], I32)
        tile_expert = sb("tile_expert", [1, MOE_TILES], I32)
        e_int = sb("e_int", [P, 2, EXPERTS], I32)

        psum = ctx.enter_context(nc.psum_tensor("psum", [P, 8, CH], F32))
        s2p = psum[:, 0:4, :].rearrange("p b (m n) -> p (b m) n", n=QB)
        S1B, AVB, MISC = 4, 6, 7
        avp = psum[:, AVB, :].rearrange("p (g n) -> p g n", g=2)
        ROW_BANKS, TURN_BANKS = (1, 2), (3, 4, 5, 6)
        Q_BANKS, K_BANKS, PRE_BANKS, V_BANKS = (0, 1), (2, 7), (3, 4), (5, 6)

        ld_x = sem("ld_x")
        ld_c = sem("ld_c")
        ld_w = sem("ld_w")
        consts = sem("consts")
        ident_ready = sem("ident_ready")
        w_turned = sem("w_turned")
        silu_done = sem("silu_done")
        mod_mm = sem("mod_mm")
        mod_steps = sem("mod_steps")
        mod_rows_done = sem("mod_rows_done")
        mod_cols_done = sem("mod_cols_done")
        scb_done = sem("scb_done")
        bn_stats_done = sem("bn_stats_done")
        bn_done = sem("bn_done")
        std_done = sem("std_done")
        rstd_done = sem("rstd_done")
        xhat_done = sem("xhat_done")
        turned = sem("turned")
        hT_done = sem("hT_done")
        proj_mm = sem("proj_mm")
        act_proj = sem("act_proj")
        dve_proj = sem("dve_proj")
        split = sem("split")
        parts_done = sem("parts_done")
        pre_scaled = sem("pre_scaled")
        store_q = sem("store_q")
        store_k = sem("store_k")
        store_pre = sem("store_pre")
        store_h = sem("store_h")
        store_pad = sem("store_pad")
        s1_done = sem("s1_done")
        ttr_done = sem("ttr_done")
        s2_done = sem("s2_done")
        exp_done = sem("exp_done")
        av_zeroed = sem("av_zeroed")
        av_done = sem("av_done")
        av_evac = sem("av_evac")
        l_done = sem("l_done")
        l_evac = sem("l_evac")
        gate_steps = sem("gate_steps")
        max_done = sem("max_done")
        c_ready = sem("c_ready")
        cT_done = sem("cT_done")
        cT_evac = sem("cT_evac")
        nT_done = sem("nT_done")
        rec_done = sem("rec_done")
        norm_done = sem("norm_done")
        work_free = sem("work_free")
        pad_zeroed = sem("pad_zeroed")
        z_part = sem("z_part")
        x_back_loaded = sem("x_back_loaded")
        h_back_loaded = sem("h_back_loaded")
        w_back = sem("w_back")
        w_mm = sem("w_mm")
        w_turn = sem("w_turn")
        sorted_zeroed = sem("sorted_zeroed")
        a_ps = sem("a_ps")
        a_sb = sem("a_sb")
        z_ps = sem("z_ps")
        z_sb = sem("z_sb")
        z_tps = sem("z_tps")
        x1_done = sem("x1_done")
        ln_stats = sem("ln_stats")
        ln_done = sem("ln_done")
        ln_std = sem("ln_std")
        ln_rstd = sem("ln_rstd")
        ln_part_done = sem("ln_part_done")
        h2_done = sem("h2_done")
        h2_ps = sem("h2_ps")
        h2T_done = sem("h2T_done")
        route_ps = sem("route_ps")
        route_step = sem("route_step")
        top_done = sem("top_done")
        exp_top = sem("exp_top")
        rows_scaled = sem("rows_scaled")
        onehot_done = sem("onehot_done")
        place_ps = sem("place_ps")
        pos_done = sem("pos_done")
        table_done = sem("table_done")
        scattered = sem("scattered")
        gate_ps = sem("gate_ps")
        up_ps = sem("up_ps")
        silu_sb = sem("silu_sb")
        act_sb = sem("act_sb")
        down_mm = sem("down_mm")
        down_sb = sem("down_sb")
        back_ps = sem("back_ps")
        acc_done = sem("acc_done")
        xT_ps = sem("xT_ps")
        xT_sb = sem("xT_sb")
        gu_ps = sem("gu_ps")
        msilu_sb = sem("msilu_sb")
        mact_sb = sem("mact_sb")
        aT_ps = sem("aT_ps")
        aT_sb = sem("aT_sb")
        y_ps = sem("y_ps")
        y_sb = sem("y_sb")
        mix_step = sem("mix_step")
        mixed = sem("mixed")
        consts2 = sem("consts2")
        out_done = sem("out_done")
        pre_loaded = [sem(f"pre_loaded{b}") for b in range(BATCH)]
        q_loaded = [[sem(f"q_loaded{b}{hf}") for hf in range(2)] for b in range(BATCH)]
        moe_loaded = [sem(f"moe_loaded{u}") for u in range(2)]
        moe_stored = [sem(f"moe_stored{u}") for u in range(2)]
        gathered = [sem(f"gathered{n}") for n in range(NG)]
        k_loaded = [sem(f"k_loaded{b}") for b in range(BATCH)]
        c_loaded = [sem(f"c_loaded{hf}") for hf in range(2)]
        block = ctx.enter_context(nc.Block())

        x_t = x.rearrange("b (t p) c -> p (b t) c", p=P)


        def pe_logits(pe, blk, j):
            t, b, i = blk
            nt, half = j // 2, j % 2
            if j == 0:
                pe.wait_ge(pre_loaded[b], (i + 1) * 16)
            else:
                pe.wait_ge(l_evac, t * 4 + j)
            pe.matmul(psum[:, MISC, :], pre_blk[:, b, nt * P:(nt + 1) * P],
                      preT[:, b, half * CH:(half + 1) * CH], start=True, stop=True).then_inc(l_done, 1)

        def act_logits(act, blk, j):
            t, b, i = blk
            nt, half = j // 2, j % 2
            act.wait_ge(l_done, t * 4 + (j + 1))
            act.activation(logits[:, b, nt, half * CH:(half + 1) * CH], psum[:, MISC, :],
                           ACT.Copy).then_inc(l_evac, 1)

        def pe_score_chunk(pe, blk, h, c, first=False):
            t, b, i = blk
            nt, half = c // 2, c % 2
            if c == 0 and h % 8 == 0:
                pe.wait_ge(q_loaded[b][h // 8], (i + 1) * 16 * Q_DMAS)
            if not (first and h == 0 and c < 2):
                pe.wait_ge(ttr_done, t * CHUNKS + (h * 4 + c - 1))
            pe.matmul(psum[:, S1B + c % 2, :], qd[0:PREV, b, h, nt * P:(nt + 1) * P],
                      kd[0:PREV, b, h, half * CH:(half + 1) * CH], start=True, stop=True).then_inc(s1_done, 1)

        def dve_max_chunk(dve, blk, h, c, chunk):
            t, b, i = blk
            nt, half = c // 2, c % 2
            if h == 0 and c == 0:
                dve.wait_ge(l_evac, t * 4 + 4)
            dve.wait_ge(s1_done, chunk)
            dve.reg_add(chunk, chunk, 1)
            dve.tensor_tensor_reduce(out=junk[:, c % 2, :], in0=psum[:, S1B + c % 2, :],
                                     in1=logits[:, b, nt, half * CH:(half + 1) * CH],
                                     scale=1.0, scalar=LOWEST, op0=ALU.add, op1=ALU.max,
                                     accum_out=row_max[:, b, h, nt, half:half + 1]).then_inc(ttr_done, 1)

        def dve_max_parts(dve, blk, hf, first=False):
            t, b, i = blk
            n = t * 2 + hf
            dve.wait_ge(ttr_done, t * CHUNKS + (hf + 1) * 32)
            if not (first and hf == 0):
                dve.wait_ge(cT_done, n)
            dve.tensor_reduce(neg_max[:, :, :], row_max[:, b, 8 * hf:8 * hf + 8, :, :], AX.X, ALU.max,
                              negate=True).then_inc(max_done, 1)
            dve.wait_ge(max_done, n * 2 + 1)
            dve.tensor_copy(c_parts[:, :, 0, :].rearrange("p t h -> p h t"), neg_max[:, :, :]).then_inc(max_done, 1)
            dve.wait_ge(max_done, n * 2 + 2)
            dve.tensor_tensor(c_parts[:, :, 1, :].rearrange("p t h -> p h t"), neg_max[:, :, :],
                              c_parts[:, :, 0, :].rearrange("p t h -> p h t"), ALU.subtract).then_inc(c_ready, 1)

        misc_b = psum[:, MISC, :].bitcast(BF16)

        def pe_max_rows(pe, blk, hf):
            t, b, i = blk
            pe.wait_ge(c_ready, t * 2 + (hf + 1))
            for nt in range(2):
                mm = pe.transpose(misc_b[0:16, nt * P:(nt + 1) * P],
                                  c_parts[:, nt, :, :].rearrange("p a h -> p (a h)"), ident_b[:, :])
            mm.then_inc(cT_done, 1)

        def act_max_rows(act, blk, hf, first=False):
            t, b, i = blk
            act.wait_ge(cT_done, t * 2 + (hf + 1))
            if not first:
                act.wait_ge(c_loaded[hf], t * 64)
            act.activation(cT[:, hf, :], misc_b[0:16, 0:QB], ACT.Copy).then_inc(cT_evac, 1)

        def sp_max_rows(sp, blk, hf):
            t, b, i = blk
            sp.wait_ge(cT_evac, t * 2 + (hf + 1))
            h0, n_next = 8 * hf, 8 - hf
            for part in range(2):
                sp.dma_start(qd[CROW + part:CROW + part + 1, b, h0:h0 + 8, :],
                             cT[8 * part:8 * part + 8, hf, :]).then_inc(c_loaded[hf], 16)
                sp.dma_start(qd[PREV + CROW + part:PREV + CROW + part + 1, b, h0 + 1:h0 + 1 + n_next, :],
                             cT[8 * part:8 * part + n_next, hf, :]).then_inc(c_loaded[hf], 16)

        def sp_load_pre(sp, b, at):
            sp.dma_start(pre_blk[:, b, :], pre_dram[b, :, bass.ds(at, QB)]).then_inc(pre_loaded[b], 16)

        def sp_load_q(sp, b, at, hf):
            n = bass.ds(at, QB)
            h0, h1 = 8 * hf, 8 * hf + 8
            p0 = max(h0, 1)
            sp.dma_start(qd[CROW:CROW + 2, b, h0:h1, :], zeros2[:, :, :]).then_inc(q_loaded[b][hf], 16)
            for slot, k in Q_RUNS:
                sp.dma_start(qd[slot * DH:(slot + k) * DH, b, h0:h1, :],
                             q_dram[b, 0:k * DH, h0:h1, n]).then_inc(q_loaded[b][hf], 16)
                sp.dma_start(qd[PREV + slot * DH:PREV + (slot + k) * DH, b, p0:h1, :],
                             q_dram[b, 0:k * DH, p0 - 1:h1 - 1, n]).then_inc(q_loaded[b][hf], 16)

        def pe_values(pe, vb, g, m):
            for j in range(GH):
                mm = pe.matmul(avp[32 * j:32 * j + DH + 1, g % 2, :], v_aug[:, vb, m, g * GH + j, :],
                               probs[:, g % 2, j, m, :], start=(m == 0), stop=(m == NT - 1),
                               skip_group_check=True)
            return mm

        def pe_norm(pe, k):
            for g in range(GROUPS):
                mm = pe.transpose(psum[:, MISC, g * P:(g + 1) * P], av_sb[:, g, k * P:(k + 1) * P], ident[:, :])
            mm.then_inc(nT_done, 1)

        def pe_block(pe, blk, first=False, last=False):
            t, b, i = blk
            for h in range(HEADS):
                g = h // GH
                for st in range(2):
                    step = 2 * h + st
                    if not last:
                        pe_score_chunk(pe, following(blk), h, 2 * st)
                    if step % 16 == 0:
                        pe.wait_ge(c_loaded[h // 8], (t + 1) * 64)
                    if not (first and h == 0):
                        pe.wait_ge(exp_done, t * STEPS + (step - 1))
                    for m in range(4 * st, 4 * st + 4):
                        keys = slice(m * P, (m + 1) * P)
                        if h == 0:
                            pe.matmul(s2p[:, m, :], preT[:, b, keys], pre_blk[:, b, :],
                                      start=(m % 2 == 0), stop=True, skip_group_check=True)
                        mm = pe.matmul(s2p[:, m, :], kd[:, b, h, keys], qd[:, b, h, :],
                                       start=False, stop=True, skip_group_check=True)
                    mm.then_inc(s2_done, 1)
                    if not last:
                        pe_score_chunk(pe, following(blk), h, 2 * st + 1)
                    if not (first and g == 0):
                        if step % 8 == 0:
                            pe.wait_ge(exp_done, t * STEPS + 8 * g)
                            if first and g == 1:
                                pe.wait_ge(av_zeroed, 1)
                            else:
                                pe.wait_ge(av_evac, t * GROUPS + (g - 1))
                        mm = pe_values(pe, b if g else 1 - b, (g - 1) % GROUPS, step % 8)
                        if step % 8 == 7:
                            mm.then_inc(av_done, 1)
                    if h == 1 and st == 1:
                        pe.wait_ge(cT_evac, t * 2 + 1)
                        pe_max_rows(pe, blk, 1)
                    if h in (2, 3) and not last:
                        if h == 2 and st == 0:
                            pe.wait_ge(cT_evac, t * 2 + 2)
                        pe_logits(pe, following(following(blk)), 2 * (h - 2) + st)
                    if h == 5 and st == 0 and not first:
                        pe.wait_ge(av_evac, t * GROUPS)
                        if last:
                            pe.wait_ge(cT_evac, t * 2 + 2)
                        else:
                            pe.wait_ge(l_evac, t * 4 + 12)
                        pe_norm(pe, 0)
                    if h == 7 and st == 0 and not first:
                        pe.wait_ge(norm_done, t * 2 - 1)
                        pe_norm(pe, 1)
                    if h == 10 and st == 0 and not last:
                        if first:
                            pe.wait_ge(l_evac, t * 4 + 12)
                        else:
                            pe.wait_ge(norm_done, t * 2)
                        pe_max_rows(pe, following(blk), 0)

        def act_values(act, blk, pg, done, first=False):
            t, b, i = blk
            act.wait_ge(av_done, done)
            if pg == 0 and not first:
                act.wait_ge(nT_done, t * 2)
            act.activation(av_sb[:, pg, :], avp[:, pg % 2, :], ACT.Copy).then_inc(av_evac, 1)

        def act_block(act, blk, first=False, last=False):
            t, b, i = blk
            for h in range(HEADS):
                g = h // GH
                for st in range(2):
                    step = 2 * h + st
                    if first and step == 0:
                        act.wait_ge(work_free, 1)
                    if step % 8 == 0 and not (first and g < 2):
                        act.wait_ge(av_done, t * GROUPS + (g - 1))
                    act.wait_ge(s2_done, t * STEPS + (step + 1))
                    act.activation(probs[:, g % 2, h % GH, 4 * st:4 * st + 4, :],
                                   s2p[:, 4 * st:4 * st + 4, :], ACT.Exp).then_inc(exp_done, 1)
                    if step % 8 == 7 and not (first and g == 0):
                        act_values(act, blk, (g - 1) % GROUPS, t * GROUPS + g, first)
                    if h == 1 and st == 1:
                        act_max_rows(act, blk, 1, first)
                    if h in (2, 3) and not last:
                        act_logits(act, following(following(blk)), 2 * (h - 2) + st)
                    if h == 10 and st == 0 and not last:
                        act_max_rows(act, following(blk), 0)

        def dve_norm(dve, blk, k):
            t, b, i = blk
            m = psum[:, MISC, :].rearrange("p (h w) -> p h w", w=32)
            dve.wait_ge(nT_done, t * 2 + (k + 1))
            dve.reciprocal(recip[:, :], m[:, :, DH]).then_inc(rec_done, 1)
            dve.wait_ge(rec_done, t * 2 + (k + 1))
            dst = attn[:, b, bass.ds(i * 2 + k, 1), :].rearrange("p o (h d) -> p (o h) d", d=DH)
            dve.tensor_tensor(dst, m[:, :, 0:DH], recip[:, :].unsqueeze(2).broadcast_to([P, HEADS, DH]),
                              ALU.mult).then_inc(norm_done, 1)

        def dve_block(dve, blk, chunk, first=False, last=False):
            for h in range(HEADS):
                if not last:
                    for c in range(4):
                        dve_max_chunk(dve, following(blk), h, c, chunk)
                    if h % 8 == 7:
                        dve_max_parts(dve, following(blk), h // 8)
                if h in (5, 7) and not first:
                    dve_norm(dve, before(blk), (h - 5) // 2)

        def sp_block(sp, blk, last=False):
            t, b, i = blk
            at = (i + 1) * QB
            if not isinstance(at, int):
                at = sp.snap(at)
            sp_max_rows(sp, blk, 1)
            if last:
                return
            sp.wait_ge(s2_done, t * STEPS + 2)
            sp_load_pre(sp, b, at)
            sp.wait_ge(s2_done, t * STEPS + 16)
            sp_load_q(sp, b, at, 0)
            sp_max_rows(sp, following(blk), 0)
            sp.wait_ge(s2_done, t * STEPS + 32)
            sp_load_q(sp, b, at, 1)

        BANK_G, BANK_U, BANK_D, BANK_B = (3, 4), (5, 6), 7, 2

        def gtiles(n):
            return slice(GRP * n, GRP * n + GRP)

        def bank_tiles(bank):
            return psum[:, bank, :].rearrange("p (t c) -> p t c", c=C)

        def turn_weights(pe):
            pe.wait_ge(w_back, 16 * 6)
            pe.wait_ge(ttr_done, BLOCKS * CHUNKS)
            for w in range(3):
                if w == 2:
                    pe.wait_ge(w_turn, 1)
                for k in range(4):
                    mm = pe.transpose(psum[:, 4 + w % 2, k * P:(k + 1) * P], w_raw[:, w, k, :], ident[:, :])
                mm.then_inc(w_mm, 1)
            pe.wait_ge(w_turn, 2)
            pe.transpose(psum[:, 5, 0:EXPERTS], r_raw, ident[0:EXPERTS, 0:EXPERTS]).then_inc(w_mm, 1)

        def copy_weights(dve):
            dve.wait_ge(s2_done, (BLOCKS - 1) * STEPS + 2)
            for w, (dst, src) in enumerate(((w_gT, psum[:, 4, :]), (w_uT, psum[:, 5, :]),
                                            (preT[:, 1, 0:SF], psum[:, 4, :]), (w_rT, psum[:, 5, 0:EXPERTS]))):
                dve.wait_ge(w_mm, w + 1)
                dve.tensor_copy(dst, src).then_inc(w_turn, 1)

        def ffn_sync(sp):
            sp.wait_ge(s2_done, (BLOCKS - 1) * STEPS)
            sp.dma_start(w_raw[:, 0, :, :], shared_gate_w.rearrange("(k p) c -> p k c", p=P)).then_inc(w_back, 16)
            sp.dma_start(w_raw[:, 1, :, :], shared_up_w.rearrange("(k p) c -> p k c", p=P)).then_inc(w_back, 16)
            sp.dma_start(w_raw[:, 2, :, :], shared_down_w.rearrange("p (k c) -> p k c", c=P)).then_inc(w_back, 16)
            sp.dma_start(r_raw, router_w).then_inc(w_back, 16)
            sp.dma_start(w_gu.rearrange("p (e f) -> p e f", e=EXPERTS),
                         gate_up_w.rearrange("e h f -> h e f")).then_inc(w_back, 16)
            sp.dma_start(w_dn.rearrange("p (e f) -> p e f", e=EXPERTS),
                         down_w.rearrange("e f h -> f e h")).then_inc(w_back, 16)
            sp.wait_ge(c_ready, 2 * BLOCKS)
            for b in range(BATCH):
                sp.dma_start(x_back[:, b, :, :], tokens[:, b * NT:(b + 1) * NT, :]).then_inc(x_back_loaded, 16)
                sp.dma_start(h_back[:, b, :], h_dram[:, b * SEQ:(b + 1) * SEQ]).then_inc(h_back_loaded, 16)
            sp.wait_ge(scattered, 16 * NTA)

            def load(c, u):
                src = sorted_dram[bass.ds(c * (GRP * P), GRP * P), :].rearrange("(t p) c -> p t c", p=P)
                sp.dma_start(moe_x[:, u, :, :], src).then_inc(moe_loaded[u], 16)

            def store(c, u):
                dst = expert_dram[bass.ds(c * (GRP * P), GRP * P), :].rearrange("(t p) c -> p t c", p=P)
                sp.wait_ge(y_sb, c + 1)
                sp.dma_start(dst, moe_y[:, u, :, :]).then_inc(moe_stored[u], 16)

            load(0, 0)
            load(1, 1)
            with sp.Fori(0, MOE_CHUNKS // 2 - 1) as k:
                for u in range(2):
                    c = k * 2 + u
                    sp.wait_ge(xT_ps, c + 1)
                    load(c + 2, u)
                    store(c, u)
            for u in range(2):
                store(MOE_CHUNKS - 2 + u, u)
            for n in range(NG):
                sp.wait_ge(mixed, n + 1)
                sp.dma_start(out_tokens[:, gtiles(n), :], acc[:, gtiles(n), :]).then_inc(out_done, 16)
            sp.wait_ge(out_done, 16 * NG)

        def ffn_pool(pool):
            pool.memset(zero_rows[:, :], 0.0).then_inc(consts2, 1)
            pool.wait_ge(consts2, 1)
            for k in range(MOE_TILES // GRP):
                pool.dma_start(sorted_dram[k * GRP * P:(k + 1) * GRP * P, :].rearrange("(t p) c -> p t c", p=P),
                               zero_rows[:, :].unsqueeze(1).broadcast_to([P, GRP, C])).then_inc(sorted_zeroed, 16)
            pool.wait_ge(av_done, BLOCKS * GROUPS)
            pool.memset(upper32, 1.0).then_inc(consts2, 1)
            pool.wait_ge(consts2, 2)
            pool.affine_select(out=upper32, in_=upper32, compare_op=ALU.is_gt, fill=0.0, base=0,
                               pattern=[[1, P]], channel_multiplier=-1).then_inc(consts2, 1)
            pool.wait_ge(consts2, 3)
            pool.tensor_copy(upper_b, upper32).then_inc(consts2, 1)
            pool.memset(ones_b, 1.0).then_inc(consts2, 1)
            pool.iota(weight_e.bitcast(I32), pattern=[[-1, EXPERTS]], base=EXPERTS,
                      channel_multiplier=0).then_inc(consts2, 1)
            pool.iota(tab_j.bitcast(I32), pattern=[[1, MOE_TILES]], base=0, channel_multiplier=0).then_inc(consts2, 1)
            pool.wait_ge(sorted_zeroed, 16 * (MOE_TILES // GRP))
            pool.wait_ge(pos_done, 1)
            for t in range(NTA):
                pool.wait_ge(rows_scaled, t // GRP + 1)
                pool.indirect_dma_start(out=sorted_dram, out_offset=bass.IndirectOffsetOnAxis(ap=pos[:, t:t + 1], axis=0),
                                        in_=rows[:, t, :], in_offset=None).then_inc(scattered, 16)
            for u in range(2):
                pool.wait_ge(moe_stored[u], 16 * (MOE_CHUNKS // 2))
            for t in range(NTA):
                pool.indirect_dma_start(out=got[:, t, :], out_offset=None, in_=expert_dram,
                                        in_offset=bass.IndirectOffsetOnAxis(ap=pos[:, t:t + 1], axis=0)
                                        ).then_inc(gathered[t // GRP], 16)

        def pe_shared(pe, n):
            cols = h2T[:, n * CH:(n + 1) * CH]
            for k in range(5):
                if k < 4:
                    u, at = k % 2, 4 * n + k
                    if at >= 2:
                        pe.wait_ge(act_sb, at - 1)
                    pe.matmul(psum[:, BANK_G[u], :], w_gT[:, k * P:(k + 1) * P], cols, start=True,
                              stop=True).then_inc(gate_ps, 1)
                    pe.matmul(psum[:, BANK_U[u], :], w_uT[:, k * P:(k + 1) * P], cols, start=True,
                              stop=True).then_inc(up_ps, 1)
                if k:
                    if k == 1 and n:
                        pe.wait_ge(down_sb, n)
                    pe.wait_ge(act_sb, 4 * n + k)
                    pe.matmul(psum[:, BANK_D, :], w_dT[:, k - 1, :], ff_act[:, (k - 1) % 2, :],
                              start=(k == 1), stop=(k == 4)).then_inc(down_mm, 1)

        def pe_shared_back(pe, n):
            pe.wait_ge(down_sb, n + 1)
            if n:
                pe.wait_ge(acc_done, n)
            for k in range(GRP):
                mm = pe.transpose(psum[:, BANK_B, k * P:(k + 1) * P], ff_out[:, n % 2, k * P:(k + 1) * P], ident[:, :])
            mm.then_inc(back_ps, 1)

        def act_shared(act, n):
            for k in range(4):
                at = 4 * n + k
                if at >= 2:
                    act.wait_ge(act_sb, at - 1)
                act.wait_ge(gate_ps, at + 1)
                act.activation(ff_silu[:, k % 2, :], psum[:, BANK_G[k % 2], :], ACT.Silu).then_inc(silu_sb, 1)
            act.wait_ge(down_mm, 4 * n + 4)
            if n >= 2:
                act.wait_ge(back_ps, n - 1)
            act.activation(ff_out[:, n % 2, :], psum[:, BANK_D, :], ACT.Identity,
                           scale=mod_cols[:, 3, n // 2:n // 2 + 1]).then_inc(down_sb, 1)

        def dve_shared(dve, n):
            for k in range(4):
                at = 4 * n + k
                if at >= 2:
                    dve.wait_ge(down_mm, at - 1)
                dve.wait_ge(silu_sb, at + 1)
                dve.wait_ge(up_ps, at + 1)
                dve.tensor_tensor(ff_act[:, k % 2, :], psum[:, BANK_U[k % 2], :], ff_silu[:, k % 2, :],
                                  ALU.mult).then_inc(act_sb, 1)

        def dve_shared_back(dve, n):
            dve.wait_ge(back_ps, n + 1)
            dve.tensor_tensor(acc[:, gtiles(n), :], bank_tiles(BANK_B), x1[:, gtiles(n), :],
                              ALU.add).then_inc(acc_done, 1)

        def pe_moe_turn(pe, c, u):
            pe.wait_ge(moe_loaded[u], (c - u) * 8 + 16)
            for k in range(GRP):
                mm = pe.transpose(psum[:, 0, k * P:(k + 1) * P], moe_x[:, u, k, :], ident[:, :])
            mm.then_inc(xT_ps, 1)

        def pe_tile_experts(pe, c):
            return [pe.value_load(tile_expert[0:1, bass.ds(c * GRP + k, 1)], min_val=0, max_val=EXPERTS - 1)
                    for k in range(GRP)]

        def pe_moe_up(pe, c):
            experts = pe_tile_experts(pe, c)
            pe.wait_ge(xT_sb, c + 1)
            for k, e in enumerate(experts):
                mm = pe.matmul(psum[:, 3 + k // 2, (k % 2) * 2 * F:(k % 2 + 1) * 2 * F], moe_xT[:, k, :],
                               w_gu[:, bass.ds(e * (2 * F), 2 * F)], start=True, stop=True)
            mm.then_inc(gu_ps, 1)

        def pe_moe_turn_act(pe, c):
            pe.wait_ge(mact_sb, c + 1)
            for k in range(GRP):
                mm = pe.transpose(psum[:, 1, k * P:(k + 1) * P], moe_act[:, k, :], ident[:, :])
            mm.then_inc(aT_ps, 1)

        def pe_moe_down(pe, c, first=False):
            experts = pe_tile_experts(pe, c)
            if not first:
                pe.wait_ge(y_sb, c)
            pe.wait_ge(aT_sb, c + 1)
            for k, e in enumerate(experts):
                mm = pe.matmul(psum[:, 5, k * P:(k + 1) * P], moe_aT[:, k, :], w_dn[:, bass.ds(e * C, C)],
                               start=True, stop=True)
            mm.then_inc(y_ps, 1)

        def act_moe_x(act, c):
            act.wait_ge(xT_ps, c + 1)
            act.activation(moe_xT, bank_tiles(0), ACT.Copy).then_inc(xT_sb, 1)

        gu_view = psum[:, 3:5, :].rearrange("p b (t f) -> p (b t) f", f=2 * F)

        def act_moe_silu(act, c, first=False):
            act.wait_ge(gu_ps, c + 1)
            if not first:
                act.wait_ge(mact_sb, c)
            act.activation(moe_silu, gu_view[:, :, 0:F], ACT.Silu).then_inc(msilu_sb, 1)

        def act_moe_y(act, c, u, first=False):
            act.wait_ge(y_ps, c + 1)
            if not first:
                act.wait_ge(moe_stored[u], (c - u) * 8)
            act.activation(moe_y[:, u, :, :], bank_tiles(5), ACT.Copy).then_inc(y_sb, 1)

        def dve_moe(dve, c):
            dve.wait_ge(msilu_sb, c + 1)
            dve.tensor_tensor(moe_act, gu_view[:, :, F:2 * F], moe_silu, ALU.mult).then_inc(mact_sb, 1)
            dve.wait_ge(aT_ps, c + 1)
            dve.tensor_copy(moe_aT, bank_tiles(1)).then_inc(aT_sb, 1)

        def ffn_pe(pe):
            def turn_attn(n):
                if n >= 2:
                    pe.wait_ge(a_sb, n - 1)
                for k in range(GRP):
                    t = GRP * n + k
                    mm = pe.transpose(psum[:, n % 2, k * P:(k + 1) * P], attn[:, t // NT, t % NT, :], ident[:, :])
                mm.then_inc(a_ps, 1)

            def project(n):
                pe.wait_ge(a_sb, n + 1)
                if n >= 2:
                    pe.wait_ge(z_sb, n - 1)
                pe.matmul(psum[:, 2 + n % 2, :], weights[:, 4, :], aT[:, n % 2, :], start=True,
                          stop=True).then_inc(z_ps, 1)

            def turn_back(n):
                pe.wait_ge(z_sb, n + 1)
                if n >= 2:
                    pe.wait_ge(x1_done, n - 1)
                for k in range(GRP):
                    mm = pe.transpose(psum[:, 4 + n % 2, k * P:(k + 1) * P], zT[:, n % 2, k * P:(k + 1) * P], ident[:, :])
                mm.then_inc(z_tps, 1)

            def turn_h2(n):
                pe.wait_ge(h2_done, GRP * (n + 1))
                if n >= 2:
                    pe.wait_ge(h2T_done, n - 1)
                for k in range(GRP):
                    mm = pe.transpose(psum[:, 6 + n % 2, k * P:(k + 1) * P], h2[:, GRP * n + k, :], ident[:, :])
                mm.then_inc(h2_ps, 1)

            def router(n):
                pe.wait_ge(h2T_done, n + 1)
                for k in range(GRP):
                    t = GRP * n + k
                    mm = pe.matmul(psum[:, 0, t * EXPERTS:(t + 1) * EXPERTS], h2T[:, t * P:(t + 1) * P], w_rT,
                                   start=True, stop=True)
                mm.then_inc(route_ps, 1)

            pe.wait_ge(norm_done, NTA)
            pe.wait_ge(w_turn, 4)
            turn_attn(0); turn_attn(1); project(0); project(1)
            turn_back(0); turn_attn(2); turn_back(1); turn_attn(3)
            project(2); project(3); turn_back(2); turn_back(3)
            turn_h2(0); turn_h2(1)
            pe.wait_ge(a_sb, NG)
            router(0); turn_h2(2); router(1); turn_h2(3); router(2); router(3)
            pe.wait_ge(x1_done, NG)
            pe.wait_ge(z_sb, NG)
            pe_shared(pe, 0)
            pe.wait_ge(onehot_done, 1)
            pe.wait_ge(consts2, 5)
            pe.matmul(psum[:, 1, 0:256], upper_b, onehot_b.rearrange("p t e -> p (t e)"), start=True, stop=False,
                      skip_group_check=True)
            for k in range(1, NTA):
                mm = pe.matmul(psum[:, 1, k * EXPERTS:256], ones_b,
                               onehot_b[:, 0:NTA - k, :].rearrange("p t e -> p (t e)"), start=False,
                               stop=(k == NTA - 1), skip_group_check=True)
            mm.then_inc(place_ps, 1)
            for k in range(NTA):
                mm = pe.matmul(psum[:, 0, 256:256 + EXPERTS], ones_b, onehot_b[:, k, :], start=(k == 0),
                               stop=(k == NTA - 1), skip_group_check=True)
            mm.then_inc(place_ps, 1)
            pe_shared_back(pe, 0)
            pe_shared(pe, 1)
            pe_shared_back(pe, 1)
            pe.wait_ge(pos_done, 1)
            pe.wait_ge(table_done, 1)
            pe.wait_ge(act_sb, 8)
            pe_moe_turn(pe, 0, 0)
            pe_moe_up(pe, 0)

            def step(c, u, first=False):
                pe_moe_turn(pe, c + 1, 1 - u)
                pe_moe_turn_act(pe, c)
                pe_moe_up(pe, c + 1)
                pe_moe_down(pe, c, first=first)

            step(0, 0, first=True)
            step(1, 1)
            with pe.Fori(1, MOE_CHUNKS // 2 - 1) as k:
                for u in range(2):
                    step(k * 2 + u, u)
            c = MOE_CHUNKS - 2
            pe_moe_turn(pe, c + 1, 1)
            pe_moe_turn_act(pe, c)
            pe_moe_up(pe, c + 1)
            pe_moe_down(pe, c)
            pe_moe_turn_act(pe, c + 1)
            pe_moe_down(pe, c + 1)
            pe.wait_ge(y_sb, MOE_CHUNKS)
            for n in (2, 3):
                pe_shared(pe, n)
                pe_shared_back(pe, n)

        def ffn_act(act):
            for n in range(NG):
                act.wait_ge(a_ps, n + 1)
                if n >= 2:
                    act.wait_ge(z_ps, n - 1)
                act.activation(aT[:, n % 2, :], psum[:, n % 2, :], ACT.Copy).then_inc(a_sb, 1)
            for n in range(NG):
                act.wait_ge(ln_done, GRP * (n + 1))
                act.activation(std[:, gtiles(n)], mv[:, gtiles(n), 1], ACT.Sqrt, bias=small[:, 0:1]).then_inc(ln_std, 1)
            for n in range(NG):
                act.wait_ge(h2_ps, n + 1)
                act.activation(h2T[:, n * CH:(n + 1) * CH], psum[:, 6 + n % 2, :], ACT.Copy).then_inc(h2T_done, 1)
            act.wait_ge(top_done, 1)
            act.activation(tok[:, 1, :], tok[:, 0, :], ACT.Exp, scale=-1.0).then_inc(exp_top, 1)
            for n in range(2):
                act_shared(act, n)
            act_moe_x(act, 0)
            act_moe_silu(act, 0, first=True)

            def step(c, u, first=False):
                act_moe_x(act, c + 1)
                act_moe_silu(act, c + 1)
                act_moe_y(act, c, u, first=first)

            for u in range(2):
                step(u, u, first=True)
            with act.Fori(1, MOE_CHUNKS // 2 - 1) as k:
                for u in range(2):
                    step(k * 2 + u, u)
            c = MOE_CHUNKS - 2
            act_moe_x(act, c + 1)
            act_moe_silu(act, c + 1)
            act_moe_y(act, c, 0)
            act_moe_y(act, c + 1, 1)
            for n in (2, 3):
                act_shared(act, n)

        def ffn_dve(dve):
            def gate_out(n):
                b = n // 2
                dve.wait_ge(z_ps, n + 1)
                if n == 0:
                    dve.wait_ge(h_back_loaded, 32)
                    dve.wait_ge(x_back_loaded, 32)
                    dve.wait_ge(av_done, BLOCKS * GROUPS)
                dve.scalar_tensor_tensor(out=zpart[:, n % 2, :], in0=psum[:, 2 + n % 2, :], scalar=small[:, 3:4],
                                         in1=h_back[:, b, (n % 2) * CH:(n % 2 + 1) * CH], op0=ALU.add,
                                         op1=ALU.add).then_inc(z_part, 1)
                dve.wait_ge(z_part, n + 1)
                if n >= 2:
                    dve.wait_ge(z_tps, n - 1)
                dve.tensor_scalar(zT[:, n % 2, :], zpart[:, n % 2, :], mod_cols[:, 2, b:b + 1], None,
                                  ALU.mult).then_inc(z_sb, 1)

            def residual(n):
                b = n // 2
                dve.wait_ge(z_tps, n + 1)
                dve.tensor_tensor(x1[:, gtiles(n), :], bank_tiles(4 + n % 2),
                                  x_back[:, b, GRP * (n % 2):GRP * (n % 2) + GRP, :], ALU.add).then_inc(x1_done, 1)
                dve.wait_ge(x1_done, n + 1)
                for k in range(GRP):
                    dve.bn_stats(stats[:, GRP * n + k, :], x1[:, GRP * n + k, :]).then_inc(ln_stats, 1)
                for k in range(GRP):
                    dve.wait_ge(ln_stats, GRP * n + k + 1)
                    dve.bn_aggr(mv[:, GRP * n + k, :], stats[:, GRP * n + k, :]).then_inc(ln_done, 1)

            def norm2(n):
                b = n // 2
                dve.wait_ge(ln_std, n + 1)
                dve.reciprocal(rstd[:, gtiles(n)], std[:, gtiles(n)]).then_inc(ln_rstd, 1)
                dve.wait_ge(ln_rstd, n + 1)
                for k in range(GRP):
                    t = GRP * n + k
                    if t >= 2:
                        dve.wait_ge(h2_done, t - 1)
                    dve.scalar_tensor_tensor(out=ln_part[:, t % 2, :], in0=x1[:, t, :], scalar=mv[:, t, 0:1],
                                             in1=mod_rows[:, b, 2, :], op0=ALU.subtract,
                                             op1=ALU.mult).then_inc(ln_part_done, 1)
                    dve.wait_ge(ln_part_done, t + 1)
                    dve.scalar_tensor_tensor(out=h2[:, t, :], in0=ln_part[:, t % 2, :], scalar=rstd[:, t:t + 1],
                                             in1=mod_rows[:, b, 1, :], op0=ALU.mult,
                                             op1=ALU.add).then_inc(h2_done, 1)

            gate_out(0); gate_out(1); residual(0); residual(1)
            gate_out(2); norm2(0); gate_out(3); residual(2); norm2(1); residual(3); norm2(2); norm2(3)

            scores = psum[:, 0, 0:256].rearrange("p (t e) -> p t e", e=EXPERTS)
            logit, is_top, ranked, onehot, place = (route[:, k, :, :] for k in range(5))
            wide = [P, NTA, EXPERTS]

            def bc(v):
                return v.unsqueeze(2).broadcast_to(wide)

            r = [0]

            def routed(ins):
                r[0] += 1
                ins.then_inc(route_step, 1)
                dve.wait_ge(route_step, r[0])

            dve.wait_ge(route_ps, NG)
            dve.wait_ge(consts2, 7)
            routed(dve.tensor_copy(weight_e, weight_e.bitcast(I32)))
            routed(dve.tensor_copy(logit, scores))
            dve.tensor_reduce(tok[:, 0, :], logit, AX.X, ALU.max).then_inc(top_done, 1)
            dve.wait_ge(top_done, 1)
            routed(dve.tensor_tensor(is_top, logit, bc(tok[:, 0, :]), ALU.is_ge))
            routed(dve.tensor_tensor(ranked, is_top, weight_e.unsqueeze(1).broadcast_to(wide), ALU.mult))
            routed(dve.tensor_reduce(tok[:, 3, :], ranked, AX.X, ALU.max))
            routed(dve.tensor_tensor(onehot, ranked, bc(tok[:, 3, :]), ALU.is_equal))
            dve.tensor_copy(onehot_b, onehot).then_inc(onehot_done, 1)
            dve.wait_ge(exp_top, 1)
            routed(dve.tensor_scalar(tok[:, 2, :], tok[:, 1, :], 1.0, None, ALU.add))
            routed(dve.reciprocal(tok[:, 4, :], tok[:, 2, :]))
            for n in range(NG):
                dve.tensor_tensor(rows[:, gtiles(n), :], h2[:, gtiles(n), :],
                                  tok[:, 4, gtiles(n)].unsqueeze(2).broadcast_to([P, GRP, C]),
                                  ALU.mult).then_inc(rows_scaled, 1)
            dve_shared(dve, 0)
            dve.wait_ge(place_ps, 2)
            routed(dve.tensor_scalar(e_int[:, 0, :], psum[:, 0, 256:256 + EXPERTS], float(P - 1), None, ALU.add))
            routed(dve.tensor_scalar(e_int[:, 1, :], e_int[:, 0, :], 7, None, ALU.arith_shift_right))
            routed(dve.tensor_copy(per_e[:, 0, :], e_int[:, 1, :]))
            routed(dve.memset(per_e[:, 1, :], 1.0))
            routed(dve.tensor_tensor_scan(per_e[:, 2, :], per_e[:, 1, :], per_e[:, 0, :], 0.0, ALU.mult, ALU.add))
            routed(dve.tensor_tensor(per_e[:, 3, :], per_e[:, 2, :], per_e[:, 0, :], ALU.subtract))
            routed(dve.tensor_scalar(per_e[:, 4, :], per_e[:, 3, :], float(P), None, ALU.mult))
            routed(dve.tensor_tensor(place, psum[:, 1, 0:256].rearrange("p (t e) -> p t e", e=EXPERTS),
                                     per_e[:, 4, :].unsqueeze(1).broadcast_to(wide), ALU.add))
            routed(dve.tensor_tensor(ranked, place, onehot, ALU.mult))
            routed(dve.tensor_reduce(tok[:, 5, :], ranked, AX.X, ALU.add))
            dve.tensor_copy(pos[:, :], tok[:, 5, :]).then_inc(pos_done, 1)
            routed(dve.tensor_copy(tab_jf, tab_j.bitcast(I32)))
            routed(dve.tensor_tensor(tab[:, 0:MOE_TILES, :], per_e[0:1, 2, :].unsqueeze(1).broadcast_to([1, MOE_TILES, EXPERTS]),
                                     tab_jf.unsqueeze(2).broadcast_to([1, MOE_TILES, EXPERTS]), ALU.is_le))
            routed(dve.tensor_reduce(tab_e, tab[:, 0:MOE_TILES, :], AX.X, ALU.add))
            dve.tensor_scalar(tile_expert[:, :], tab_e, float(EXPERTS - 1), None, ALU.min).then_inc(table_done, 1)
            dve_shared_back(dve, 0)
            dve_shared(dve, 1)
            dve_shared_back(dve, 1)
            with dve.Fori(0, MOE_CHUNKS) as c:
                dve_moe(dve, c)
            for n in (2, 3):
                dve_shared(dve, n)
                dve_shared_back(dve, n)
            for n in range(NG):
                b = n // 2
                dve.wait_ge(gathered[n], 16 * GRP)
                dve.tensor_tensor(got[:, gtiles(n), :], got[:, gtiles(n), :],
                                  mod_rows[:, b, 3, :].unsqueeze(1).broadcast_to([P, GRP, C]),
                                  ALU.mult).then_inc(mix_step, 1)
                dve.wait_ge(mix_step, n + 1)
                dve.wait_ge(acc_done, n + 1)
                dve.tensor_tensor(acc[:, gtiles(n), :], acc[:, gtiles(n), :], got[:, gtiles(n), :],
                                  ALU.add).then_inc(mixed, 1)

        out_tokens = out.rearrange("b (t p) c -> p (b t) c", p=P)
        tokens = x.rearrange("b (t p) c -> p (b t) c", p=P)

        @block.sync
        def _(sp):
            for b in range(BATCH):
                sp.dma_start(xs[:, b * NT:(b + 1) * NT, :], tokens[:, b * NT:(b + 1) * NT, :]).then_inc(ld_x, 16)
            for b in range(BATCH):
                for w, (dram, done) in enumerate(((q_dram, store_q), (k_dram, store_k), (nk_dram, store_k))):
                    sp.wait_ge(parts_done, 3 * b + w + 1)
                    for part in range(3):
                        sp.dma_start(dram[b, part * DH:(part + 1) * DH, :, 0:SEQ].rearrange("d h n -> (d h) n"),
                                     parts[:, w, part, :]).then_inc(done, 16)
                sp.wait_ge(pre_scaled, b + 1)
                sp.dma_start(pre_dram[b, :, 0:SEQ], preS).then_inc(store_pre, 16)
                sp.wait_ge(hT_done, 2 * b + 2)
                sp.dma_start(h_dram[:, b * SEQ:(b + 1) * SEQ], hT[:, b, :]).then_inc(store_h, 16)
                sp.wait_ge(store_pre, 16 * (b + 1))
                sp_load_pre(sp, b, 0)
                sp.wait_ge(store_q, 48 * (b + 1))
                sp.wait_ge(consts, 7)
                for hf in range(2):
                    sp_load_q(sp, b, 0, hf)
                sp.wait_ge(store_k, 96 * (b + 1))
                for slot, part in enumerate(K_PART):
                    rows = slice(part * DH, (part + 1) * DH)
                    sp.dma_start(kd[slot * DH:(slot + 1) * DH, b, :, :], k_dram[b, rows, :, :]).then_inc(k_loaded[b], 16)
                    sp.dma_start(kd[PREV + slot * DH:PREV + (slot + 1) * DH, b, 1:, :],
                                 nk_dram[b, rows, 0:HEADS - 1, :]).then_inc(k_loaded[b], 16)
            sp.wait_ge(store_pad, 64)
            sp_max_rows(sp, (0, 0, 0), 0)
            sp_block(sp, (0, 0, 0))
            with sp.Fori(0, LOOPS) as k:
                sp_block(sp, (k * 2 + 1, 1, k))
                sp_block(sp, (k * 2 + 2, 0, k + 1))
            sp_block(sp, (BLOCKS - 1, 1, NT // 2 - 1), last=True)
            ffn_sync(sp)
            for hf in range(2):
                sp.wait_ge(q_loaded[0][hf], (NT // 2 + 1) * 16 * Q_DMAS)
        @block.gpsimd
        def _(pool):
            pool.memset(small[:, 0:1], EPS).then_inc(consts, 1)
            pool.memset(ident[:, :], 0.0).then_inc(ident_ready, 1)
            pool.wait_ge(ident_ready, 1)
            pool.affine_select(out=ident[:, :], in_=ident[:, :], compare_op=ALU.not_equal, fill=1.0, base=0,
                               pattern=[[-1, P]], channel_multiplier=1).then_inc(ident_ready, 1)
            pool.wait_ge(ident_ready, 2)
            pool.tensor_copy(ident_b[:, :], ident[:, :]).then_inc(ident_ready, 1)
            pool.wait_ge(ld_w, 128)
            pool.tensor_copy(w_dh.rearrange("p w (d h) -> p w d h", d=DH),
                             weights[:, 0:2, :].rearrange("p w (h d) -> p w d h", d=DH)).then_inc(w_turned, 1)
            pool.wait_ge(w_turned, 1)
            fills = ((zeros2[:, :, :], 0.0),
                     (kd[32:64, :, :, :].bitcast(F32), ONE_PAIR),
                     (kd[96:128, :, :, :].bitcast(F32), MINUS_ONE_PAIR),
                     (qd[32:64, :, :, :].bitcast(F32), 0.0),
                     (qd[64:128, :, :, :].bitcast(F32), 0.0),
                     (kd[64:128, :, 0, :].bitcast(F32), 0.0),
                     (v_aug[:, :, :, :, :], 1.0))
            for n, (tile, value) in enumerate(fills):
                pool.wait_ge(consts, n + 1)
                pool.memset(tile, value).then_inc(consts, 1)
            pool.wait_ge(consts, 8)
            pool.memset(attn[:, 0, 0:3, :], 0.0).then_inc(pad_zeroed, 1)
            pool.wait_ge(pad_zeroed, 1)
            zeros = attn[:, 0, 0:3, :].rearrange("p t c -> p (t c)")
            pool.dma_start(pre_dram[0, :, SEQ:PAD], zeros[:, 0:QB]).then_inc(store_pad, 16)
            for part in range(3):
                pool.dma_start(q_dram[0, part * DH:(part + 1) * DH, :, SEQ:PAD].rearrange("d h n -> (d h) n"),
                               zeros.bitcast(BF16)[:, part * QB:(part + 1) * QB]).then_inc(store_pad, 16)
            pool.wait_ge(store_q, 96)
            pool.wait_ge(store_k, 192)
            pool.wait_ge(store_pre, 32)
            pool.wait_ge(store_h, 32)
            pool.wait_ge(proj_mm, 16)
            pool.wait_ge(pre_scaled, 2)
            pool.memset(small[:, 7:8], 0.0).then_inc(work_free, 1)
            ffn_pool(pool)

        @block.tensor
        def _(pe):
            pe.wait_ge(ld_c, 32)
            pe.wait_ge(silu_done, 1)
            for n, k in enumerate((0, 1, 2, 5)):
                mm = pe.matmul(psum[:, 0, 2 * n:2 * n + 2], wmod_sb[:, k * C:(k + 1) * C], silu_c[:, :],
                               start=True, stop=True)
            mm.then_inc(mod_mm, 1)
            pe.wait_ge(scb_done, BATCH)
            for b in range(BATCH):
                pe.matmul(psum[:, ROW_BANKS[b], :], silu_cb[:, b, :], wmod_sb[:, 2 * C:6 * C],
                          start=True, stop=True).then_inc(mod_mm, 1)
            pe.wait_ge(ident_ready, 3)
            for n, bank in enumerate(TURN_BANKS):
                pe.wait_ge(xhat_done, 4 * n + 4)
                for k in range(4):
                    mm = pe.transpose(psum[:, bank, k * P:(k + 1) * P], xhat[:, 4 * n + k, :], ident[:, :])
                mm.then_inc(turned, 1)
            pe.wait_ge(ld_w, 128)
            pe.wait_ge(mod_cols_done, 3)
            pe.wait_ge(mod_rows_done, 2 * 4)
            pe.wait_ge(w_turned, 1)
            for b in range(BATCH):
                for half in range(2):
                    cols = hT[:, b, half * CH:(half + 1) * CH]
                    pe.wait_ge(hT_done, 2 * b + half + 1)
                    if b:
                        pe.wait_ge(act_proj, half + 1)
                    pe.matmul(psum[:, Q_BANKS[half], :], w_dh[:, 0, :], cols, start=True, stop=True).then_inc(proj_mm, 1)
                for half in range(2):
                    cols = hT[:, b, half * CH:(half + 1) * CH]
                    if b:
                        pe.wait_ge(dve_proj, half + 1)
                    pe.matmul(psum[:, K_BANKS[half], :], w_dh[:, 1, :], cols, start=True, stop=True).then_inc(proj_mm, 1)
                for half in range(2):
                    cols = hT[:, b, half * CH:(half + 1) * CH]
                    if b:
                        pe.wait_ge(act_proj, half + 3)
                    else:
                        pe.wait_ge(hT_done, half + 1)
                    pe.matmul(psum[:, PRE_BANKS[half], :], weights[:, 3, :], cols, start=True,
                              stop=True).then_inc(proj_mm, 1)
                for half in range(2):
                    if b:
                        pe.wait_ge(dve_proj, half + 3)
                    else:
                        pe.wait_ge(hT_done, half + 3)
                    for k in range(4):
                        at = half * CH + k * P
                        mm = pe.matmul(psum[:, V_BANKS[half], k * P:(k + 1) * P], hT[:, b, at:at + P],
                                       weights[:, 2, :], start=True, stop=True)
                    mm.then_inc(proj_mm, 1)
            pe.wait_ge(act_proj, 8)
            pe.wait_ge(dve_proj, 8)
            for j in range(4):
                pe_logits(pe, (0, 0, 0), j)
            pe.wait_ge(k_loaded[0], 192)
            for h in range(HEADS):
                for c in range(4):
                    pe_score_chunk(pe, (0, 0, 0), h, c, first=True)
                if h == 2:
                    pe.wait_ge(l_evac, 4)
                    for j in range(4):
                        pe_logits(pe, (1, 1, 0), j)
                if h == 10:
                    pe.wait_ge(l_evac, 8)
                    pe_max_rows(pe, (0, 0, 0), 0)
            pe.wait_ge(k_loaded[1], 192)
            pe_block(pe, (0, 0, 0), first=True)
            with pe.Fori(0, LOOPS) as k:
                pe_block(pe, (k * 2 + 1, 1, k))
                pe_block(pe, (k * 2 + 2, 0, k + 1))
            pe_block(pe, (BLOCKS - 1, 1, NT // 2 - 1), last=True)
            turn_weights(pe)
            pe.wait_ge(exp_done, BLOCKS * STEPS)
            pe.wait_ge(av_evac, BLOCKS * GROUPS - 1)
            for m in range(NT):
                mm = pe_values(pe, 1, GROUPS - 1, m)
            mm.then_inc(av_done, 1)
            pe.wait_ge(av_evac, BLOCKS * GROUPS)
            for k in range(2):
                pe.wait_ge(norm_done, 2 * BLOCKS - 2 + k)
                pe_norm(pe, k)
            ffn_pe(pe)

        @block.scalar
        def _(act):
            act.dma_start(silu_in[:, :], cond.rearrange("b c -> c b"), allow_slow_non_contiguous=True).then_inc(ld_c, 16)
            act.dma_start(wmod_sb, wmod).then_inc(ld_c, 16)
            for n, w in enumerate((wq, wk, wv, wpre, wproj)):
                act.dma_start(weights[:, n, :], w).then_inc(ld_w, 16)
            act.dma_start(small[:, 1:2], bpre.rearrange("(c o) -> c o", o=1)).then_inc(ld_w, 16)
            act.dma_start(small[:, 3:4], bproj.rearrange("(c o) -> c o", o=1)).then_inc(ld_w, 16)
            act.dma_start(small[:, 2:3], pi.partition_broadcast(P)).then_inc(ld_w, 16)
            act.wait_ge(ld_c, 32)
            act.activation(silu_c[:, :], silu_in[:, :], ACT.Silu).then_inc(silu_done, 1)
            act.wait_ge(bn_done, NTA)
            act.wait_ge(consts, 1)
            act.activation(std[:, :], mv[:, :, 1], ACT.Sqrt, bias=small[:, 0:1]).then_inc(std_done, 1)
            act.wait_ge(mod_cols_done, 3)
            for n, bank in enumerate(TURN_BANKS):
                b, half = n // 2, n % 2
                act.wait_ge(turned, n + 1)
                act.activation(hT[:, b, half * CH:(half + 1) * CH], psum[:, bank, :], ACT.Identity,
                               bias=mod_cols[:, 0, b:b + 1], scale=mod_cols[:, 1, b:b + 1]).then_inc(hT_done, 1)
            act.wait_ge(ld_w, 128)
            for b in range(BATCH):
                if b:
                    act.wait_ge(parts_done, 1)
                for half in range(2):
                    act.wait_ge(proj_mm, 8 * b + half + 1)
                    act.activation(qk32[:, 0, half * CH:(half + 1) * CH], psum[:, Q_BANKS[half], :], ACT.Copy,
                                   scale=float(DH) ** -0.5).then_inc(act_proj, 1)
                for half in range(2):
                    act.wait_ge(proj_mm, 8 * b + half + 5)
                    act.activation(preT[:, b, half * CH:(half + 1) * CH], psum[:, PRE_BANKS[half], :], ACT.Silu,
                                   bias=small[:, 1:2]).then_inc(act_proj, 1)
            for t in range(2):
                for j in range(4):
                    act_logits(act, (t, t, 0), j)
            act_max_rows(act, (0, 0, 0), 0, first=True)
            act_block(act, (0, 0, 0), first=True)
            with act.Fori(0, LOOPS) as k:
                act_block(act, (k * 2 + 1, 1, k))
                act_block(act, (k * 2 + 2, 0, k + 1))
            act_block(act, (BLOCKS - 1, 1, NT // 2 - 1), last=True)
            act_values(act, (BLOCKS, 0, 0), GROUPS - 1, BLOCKS * GROUPS)
            ffn_act(act)

        @block.vector
        def _(dve):
            for t in range(NTA):
                if t % NT == 0:
                    dve.wait_ge(ld_x, 32)
                dve.bn_stats(stats[:, t, :], xs[:, t, :]).then_inc(bn_stats_done, 1)
            for t in range(NTA):
                dve.wait_ge(bn_stats_done, t + 1)
                dve.bn_aggr(mv[:, t, :], stats[:, t, :]).then_inc(bn_done, 1)
            dve.wait_ge(silu_done, 1)
            for b in range(BATCH):
                dve.tensor_copy(silu_cb[:, b, :], silu_c[:, b:b + 1].broadcast_to([P, P])).then_inc(scb_done, 1)
            dve.wait_ge(std_done, 1)
            dve.reciprocal(rstd[:, :], std[:, :]).then_inc(rstd_done, 1)
            dve.wait_ge(rstd_done, 1)
            for t in range(NTA):
                dve.tensor_scalar(xhat[:, t, :], xs[:, t, :], mv[:, t, 0:1], rstd[:, t:t + 1], ALU.subtract,
                                  ALU.mult).then_inc(xhat_done, 1)
            dve.wait_ge(mod_mm, 1)
            dve.tensor_copy(mod_cols[:, 0, :], psum[:, 0, 0:2]).then_inc(mod_cols_done, 1)
            dve.tensor_scalar(mod_cols[:, 1, :], psum[:, 0, 2:4], 1.0, None, ALU.add).then_inc(mod_cols_done, 1)
            dve.tensor_scalar(gate_cols[:, 0, :], psum[:, 0, 4:8], 0.0, 2.0, ALU.is_ge, ALU.mult).then_inc(gate_steps, 1)
            dve.wait_ge(gate_steps, 1)
            dve.tensor_scalar(gate_cols[:, 1, :], gate_cols[:, 0, :], -1.0, None, ALU.add).then_inc(gate_steps, 1)
            dve.scalar_tensor_tensor(out=gate_cols[:, 2, :], in0=gate_cols[:, 0, :], scalar=-1.0, in1=psum[:, 0, 4:8],
                                     op0=ALU.add, op1=ALU.mult).then_inc(gate_steps, 1)
            dve.wait_ge(gate_steps, 3)
            dve.scalar_tensor_tensor(out=mod_cols[:, 2:4, :].rearrange("p k b -> p (k b)"), in0=gate_cols[:, 2, :],
                                     scalar=0.25, in1=gate_cols[:, 1, :], op0=ALU.max,
                                     op1=ALU.mult).then_inc(mod_cols_done, 1)
            dve.wait_ge(mod_mm, 3)
            for b in range(BATCH):
                src = psum[:, ROW_BANKS[b], :].rearrange("p (k c) -> p k c", k=4)
                dve.tensor_copy(mod_rows[:, b, 1, :], src[:, 1, :]).then_inc(mod_rows_done, 1)
                dve.tensor_scalar(mod_rows[:, b, 2, :], src[:, 2, :], 1.0, None, ALU.add).then_inc(mod_rows_done, 1)
                for k in (0, 3):
                    n = 2 * b + k // 3
                    dve.tensor_scalar(gate_step[:, n, :], src[:, k, :], 0.0, 2.0, ALU.is_ge,
                                      ALU.mult).then_inc(mod_steps, 1)
                    dve.wait_ge(mod_steps, 3 * n + 1)
                    dve.tensor_scalar(gate_sign[:, n, :], gate_step[:, n, :], -1.0, None, ALU.add).then_inc(mod_steps, 1)
                    dve.scalar_tensor_tensor(out=gate_size[:, n, :], in0=gate_step[:, n, :], scalar=-1.0,
                                             in1=src[:, k, :], op0=ALU.add, op1=ALU.mult).then_inc(mod_steps, 1)
                    dve.wait_ge(mod_steps, 3 * n + 3)
                    dve.scalar_tensor_tensor(out=mod_rows[:, b, k, :], in0=gate_size[:, n, :], scalar=0.25,
                                             in1=gate_sign[:, n, :], op0=ALU.max,
                                             op1=ALU.mult).then_inc(mod_rows_done, 1)
            dve.wait_ge(mod_rows_done, 8)
            dve.wait_ge(consts, 8)
            for b in range(BATCH):
                if b:
                    dve.wait_ge(parts_done, 2)
                for half in range(2):
                    dve.wait_ge(proj_mm, 8 * b + half + 3)
                    dve.tensor_copy(qk32[:, 1, half * CH:(half + 1) * CH],
                                    psum[:, K_BANKS[half], :]).then_inc(dve_proj, 1)
                for half in range(2):
                    dve.wait_ge(proj_mm, 8 * b + half + 7)
                    dve.tensor_copy(v_aug[:, b, 4 * half:4 * half + 4, :, 0:DH],
                                    psum[:, V_BANKS[half], :].rearrange("p (t h d) -> p t h d", t=4, d=DH)
                                    ).then_inc(dve_proj, 1)
                if b:
                    dve.wait_ge(store_q, 48)
                    dve.wait_ge(store_k, 96)
                for w in range(2):
                    if w == 0:
                        dve.wait_ge(act_proj, 4 * b + 2)
                    else:
                        dve.wait_ge(dve_proj, 4 * b + 2)
                    n = 3 * (2 * b + w)
                    if b:
                        dve.wait_ge(parts_done, 3)
                    dve.tensor_copy(parts[:, w, 0, :], qk32[:, w, :]).then_inc(split, 1)
                    dve.wait_ge(split, n + 1)
                    dve.tensor_tensor(rest[:, w, :], qk32[:, w, :], parts[:, w, 0, :], ALU.subtract).then_inc(split, 1)
                    dve.wait_ge(split, n + 2)
                    dve.tensor_copy(parts[:, w, 1, :], rest[:, w, :]).then_inc(split, 1)
                    dve.wait_ge(split, n + 3)
                    dve.tensor_tensor(parts[:, w, 2, :], rest[:, w, :], parts[:, w, 1, :],
                                      ALU.subtract).then_inc(parts_done, 1)
                dve.wait_ge(parts_done, 3 * b + 2)
                dve.tensor_scalar(parts[:, 2, :, :], parts[:, 1, :, :], -1.0, None, ALU.mult).then_inc(parts_done, 1)
                dve.wait_ge(act_proj, 4 * b + 4)
                if b:
                    dve.wait_ge(store_pre, 16)
                dve.tensor_scalar(preS, preT[:, b, :], small[:, 2:3], float(C) ** -0.5, ALU.mult,
                                  ALU.mult).then_inc(pre_scaled, 1)
            dve.memset(psum[:, AVB, :], 0.0).then_inc(av_zeroed, 1)
            dve.wait_ge(store_pad, 64)
            chunk = dve.alloc_register("next_score_chunk")
            dve.reg_mov(chunk, 1)
            for h in range(HEADS):
                for c in range(4):
                    dve_max_chunk(dve, (0, 0, 0), h, c, chunk)
                if h % 8 == 7:
                    dve_max_parts(dve, (0, 0, 0), h // 8, first=True)
            dve_block(dve, (0, 0, 0), chunk, first=True)
            with dve.Fori(0, LOOPS) as k:
                dve_block(dve, (k * 2 + 1, 1, k), chunk)
                dve_block(dve, (k * 2 + 2, 0, k + 1), chunk)
            dve_block(dve, (BLOCKS - 1, 1, NT // 2 - 1), chunk, last=True)
            copy_weights(dve)
            for k in range(2):
                dve_norm(dve, (BLOCKS - 1, 1, NT // 2 - 1), k)
            ffn_dve(dve)


_INPUTS = ("L0_attn_x", "L0_attn_Wq", "L0_attn_Wk", "L0_attn_Wv", "L0_attn_Wproj", "L0_attn_bproj",
           "L0_attn_Wpre", "L0_attn_bpre", "L0_attn_pi", "L0_c", "L0_wmod", "L0_ffn_router_w",
           "L0_ffn_gate_up_proj", "L0_ffn_down_proj", "L0_ffn_shared_gate_w", "L0_ffn_shared_up_w",
           "L0_ffn_shared_down_w")


def kernel(**inputs):
    import concourse.bacc as bacc
    from concourse.bass_utils import run_bass_kernel_spmd

    nc = bacc.Bacc("TRN2", target_bir_lowering=False, num_devices=1)
    arrays, args = {}, []
    for name in _INPUTS:
        a = np.ascontiguousarray(inputs[name])
        arrays[name] = a
        args.append(nc.dram_tensor(name, a.shape, mybir.dt.from_np(a.dtype), kind="ExternalInput").ap())
    shape = arrays["L0_attn_x"].shape
    args.append(nc.dram_tensor("out", shape, F32, kind="ExternalOutput").ap())
    build(nc, *args)
    return run_bass_kernel_spmd(nc, [arrays], core_ids=[0]).results[0]["out"]
```

```python
from contextlib import ExitStack

import numpy as np

import concourse.bass as bass
from concourse import mybir

F32 = mybir.dt.float32
BF16 = mybir.dt.bfloat16
I32 = mybir.dt.int32
ALU = mybir.AluOpType
ACT = mybir.ActivationFunctionType
AX = mybir.AxisListType

P = 128
C = 128
HEADS = 16
DH = C // HEADS
BATCH = 2
SEQ = 1024
NT = SEQ // P
NTA = BATCH * NT
QB = 256
BLOCKS = BATCH * SEQ // QB
PAD = SEQ + QB
CH = 512
GH = 4
GROUPS = HEADS // GH
EPS = 1e-5
LOWEST = -3.0e38
Q_PART = (0, 1, 2, 0, 1, 0)
K_PART = (0, 0, 0, 1, 1, 2)
ROWS = 6 * DH
CROW = ROWS
PREV = 64
LEAD = 11
CHUNKS = HEADS * 4
STEPS = HEADS * 2
EXPERTS = 16
F = 128
SF = 512
MOE_TILES = NTA + EXPERTS
MOE_CHUNKS = MOE_TILES // 4
GRP = 4
NG = NTA // GRP
Q_RUNS = ((0, 3), (3, 2), (5, 1))
Q_DMAS = 2 * len(Q_RUNS) + 1
ONE_PAIR = float(np.array([0x3F803F80], np.uint32).view(np.float32)[0])
MINUS_ONE_PAIR = float(np.array([0xBF80BF80], np.uint32).view(np.float32)[0])


LOOPS = (BLOCKS - 2) // 2


def following(blk):
    t, b, i = blk
    return t + 1, 1 - b, i + b


def before(blk):
    t, b, i = blk
    return t - 1, 1 - b, i - (1 - b)


def build(nc, x, wq, wk, wv, wproj, bproj, wpre, bpre, pi, cond, wmod,
          router_w, gate_up_w, down_w, shared_gate_w, shared_up_w, shared_down_w, out):
    with ExitStack() as ctx:
        def sb(name, shape, dt=F32):
            return ctx.enter_context(nc.sbuf_tensor(name, shape, dt))

        def sem(name):
            return ctx.enter_context(nc.semaphore(name))

        q_dram = nc.dram_tensor("q_parts", [BATCH, 3 * DH, HEADS, PAD], BF16).ap()
        pre_dram = nc.dram_tensor("pre_scaled", [BATCH, P, PAD], F32).ap()
        sorted_dram = nc.dram_tensor("sorted_tokens", [MOE_TILES * P, C], F32).ap()
        expert_dram = nc.dram_tensor("expert_outputs", [MOE_TILES * P, C], F32).ap()
        h_dram = nc.dram_tensor("h_cols", [P, BATCH * SEQ], F32).ap()

        kd_flat = sb("kd", [P, (BATCH * HEADS + 1) * SEQ], BF16)
        kd = kd_flat[:, 0:BATCH * HEADS * SEQ].rearrange("p (b h n) -> p b h n", b=BATCH, h=HEADS)
        qd = sb("qd", [P, 2, HEADS, QB], BF16)
        work = sb("work", [P, 2 * GH * NT * QB])
        probs = work[:, :].rearrange("p (s h m n) -> p s h m n", s=2, h=GH, m=NT)
        v_aug = sb("v_aug", [P, BATCH, NT, HEADS, DH + 1])
        preT = sb("preT", [P, BATCH, SEQ])
        pre_blk = sb("pre_blk", [P, 2, QB])
        logits = sb("logits", [P, 2, 2, SEQ])
        av_sb = sb("av_sb", [P, GROUPS, QB])
        attn = sb("attn", [P, BATCH, NT, C])
        junk = sb("junk", [P, 2, CH], BF16)
        row_max = sb("row_max", [P, 2, HEADS, 2, 2])
        neg_max = sb("neg_max", [P, 8, 2])
        c_parts = sb("c_parts", [P, 2, 2, 8], BF16)
        cT = sb("cT", [16, 2, QB], BF16)
        recip = sb("recip", [P, HEADS])
        ident = sb("ident", [P, P])
        ident_b = sb("ident_b", [P, P], BF16)
        zeros2 = sb("zeros2", [2, QB], BF16)
        weights = sb("weights", [P, 5, C])
        mod_cols = sb("mod_cols", [P, 4, BATCH])
        gate_cols = sb("gate_cols", [P, 3, 2 * BATCH])
        mod_rows = sb("mod_rows", [P, BATCH, 3, C])
        small = sb("small", [P, 8])
        stats = sb("stats", [P, NTA, 6])
        mv = sb("mv", [P, NTA, 2])
        std = sb("std", [P, NTA])
        rstd = sb("rstd", [P, NTA])
        silu_in = sb("silu_in", [P, BATCH])
        silu_c = sb("silu_c", [P, BATCH])

        def view(at, n):
            return work[:, at:at + n]

        xs = view(0, 2048).rearrange("p (t c) -> p t c", t=NTA)
        xhat = view(2048, 2048).rearrange("p (t c) -> p t c", t=NTA)
        hT = view(4096, 2048).rearrange("p (b n) -> p b n", b=BATCH)
        qk32 = view(6144, 2048).rearrange("p (w n) -> p w n", w=2)
        rest = view(8192, 2048).rearrange("p (w n) -> p w n", w=2)
        wmod_sb = view(8192, 768)
        preS = view(14848, 1024)
        w_dh = view(16128, 256).rearrange("p (w n) -> p w n", w=2)

        def parts_at(area):
            return area.bitcast(BF16).rearrange("p (s n) -> p s n", s=3)

        parts = ((parts_at(view(10240, 1536)), parts_at(view(11776, 1536)), parts_at(view(13312, 1536))),
                 (parts_at(logits[:, 1, :, :].rearrange("p t n -> p (t n)")[:, 0:1536]),
                  parts_at(view(0, 1536)), parts_at(view(1536, 1536))))

        kd32 = [kd[:, b, :, :].rearrange("p h n -> p (h n)").bitcast(F32) for b in range(BATCH)]
        w_gu = kd32[0][:, 0:4096]
        w_dn = kd32[0][:, 4096:6144]
        w_raw = kd32[0][:, 6144:7680].rearrange("p (w k c) -> p w k c", w=3, k=4)
        r_raw = kd32[0][0:EXPERTS, 7680:7808]
        x_back = logits[:, :, 0, :].rearrange("p b (t c) -> p b t c", c=C)
        h_back = logits[:, :, 1, :]
        w_gT = preT[:, 0, 0:SF]
        w_uT = preT[:, 0, SF:2 * SF]
        w_dT = preT[:, 1, 0:SF].rearrange("p (k c) -> p k c", k=4)
        w_rT = preT[:, 1, SF:SF + EXPERTS]
        silu_cb = preT[:, 1, SF + 16:SF + 272].rearrange("p (b c) -> p b c", b=BATCH)
        wmod_rows = kd32[0][:, 7808:8192]
        gate_step = junk[:, 0, :].bitcast(F32)[:, 0:C]
        gate_sign = junk[:, 0, :].bitcast(F32)[:, C:2 * C]
        gate_size = junk[:, 1, :].bitcast(F32)[:, 0:C]
        aT = view(0, 1024).rearrange("p (u n) -> p u n", u=2)
        zT = view(1024, 1024).rearrange("p (u n) -> p u n", u=2)
        x1 = view(2048, 2048).rearrange("p (t c) -> p t c", t=NTA)
        h2 = view(4096, 2048).rearrange("p (t c) -> p t c", t=NTA)
        h2T = view(6144, 2048)
        acc = view(8192, 2048).rearrange("p (t c) -> p t c", t=NTA)
        ff_silu = view(10240, 1024).rearrange("p (u n) -> p u n", u=2)
        ff_act = view(11264, 1024).rearrange("p (u n) -> p u n", u=2)
        ff_out = view(12288, 1024).rearrange("p (u n) -> p u n", u=2)
        zpart = ff_silu
        ln_part = view(13312, 256).rearrange("p (u n) -> p u n", u=2)
        route = view(13568, 5 * 256).rearrange("p (k t e) -> p k t e", k=5, t=NTA)
        onehot_b = view(14848, 128).bitcast(BF16).rearrange("p (t e) -> p t e", t=NTA)
        upper_b = view(14976, 64).bitcast(BF16)
        ones_b = view(15040, 64).bitcast(BF16)
        tok = view(15104, 128).rearrange("p (k t) -> p k t", k=8)
        per_e = view(15232, 128).rearrange("p (k e) -> p k e", k=8)
        weight_e = view(15360, 16)
        upper32 = view(15376, 128)
        tab = work[0:1, 15504:15504 + MOE_TILES * EXPERTS].rearrange("p (j e) -> p j e", e=EXPERTS)
        tab_j = work[0:1, 16016:16016 + MOE_TILES]
        tab_jf = work[0:1, 16048:16048 + MOE_TILES]
        tab_e = work[0:1, 16080:16080 + MOE_TILES]
        rows = kd32[1][:, 0:2048].rearrange("p (t c) -> p t c", t=NTA)
        moe_x = kd32[1][:, 2048:3072].rearrange("p (u t c) -> p u t c", u=2, t=GRP)
        moe_xT = kd32[1][:, 3072:3584].rearrange("p (t n) -> p t n", t=GRP)
        moe_silu = kd32[1][:, 3584:4096].rearrange("p (t n) -> p t n", t=GRP)
        moe_act = kd32[1][:, 4096:4608].rearrange("p (t n) -> p t n", t=GRP)
        moe_aT = kd32[1][:, 4608:5120].rearrange("p (t n) -> p t n", t=GRP)
        moe_y = kd32[1][:, 5120:6144].rearrange("p (u t c) -> p u t c", u=2, t=GRP)
        got = kd32[1][:, 6144:8192].rearrange("p (t c) -> p t c", t=NTA)
        zero_rows = sb("zero_rows", [P, C])
        pos = sb("pos", [P, NTA], I32)
        tile_expert = sb("tile_expert", [1, MOE_TILES], I32)
        e_int = sb("e_int", [P, 2, EXPERTS], I32)

        psum = ctx.enter_context(nc.psum_tensor("psum", [P, 8, CH], F32))
        s2p = psum[:, 0:4, :].rearrange("p b (m n) -> p (b m) n", n=QB)
        S1B, AVB, MISC = 4, 6, 7
        avp = psum[:, AVB, :].rearrange("p (g n) -> p g n", g=2)
        TURN_BANKS = ((3, 4), (5, 6))
        Q_BANKS, K_BANKS, PRE_BANKS, V_BANKS = ((0, 1), (0, 1)), ((2, 7), (2, 3)), ((3, 4), (0, 1)), ((5, 6), (2, 3))

        ld_c = sem("ld_c")
        ld_w = sem("ld_w")
        consts = sem("consts")
        ident_ready = sem("ident_ready")
        w_turned = sem("w_turned")
        pi_scaled = sem("pi_scaled")
        silu_done = sem("silu_done")
        mod_mm = sem("mod_mm")
        mod_rows_mm = sem("mod_rows_mm")
        mod_steps = sem("mod_steps")
        mod_rows_done = sem("mod_rows_done")
        mod_cols_done = sem("mod_cols_done")
        scb_done = sem("scb_done")
        store_pad = sem("store_pad")
        s1_done = sem("s1_done")
        ttr_done = sem("ttr_done")
        s2_done = sem("s2_done")
        exp_done = sem("exp_done")
        av_zeroed = sem("av_zeroed")
        av_done = sem("av_done")
        av_evac = sem("av_evac")
        l_done = sem("l_done")
        l_evac = sem("l_evac")
        gate_steps = sem("gate_steps")
        max_done = sem("max_done")
        c_ready = sem("c_ready")
        cT_done = sem("cT_done")
        cT_evac = sem("cT_evac")
        nT_done = sem("nT_done")
        rec_done = sem("rec_done")
        norm_done = sem("norm_done")
        pad_zeroed = sem("pad_zeroed")
        z_part = sem("z_part")
        x_back_loaded = sem("x_back_loaded")
        h_back_loaded = sem("h_back_loaded")
        w_back = sem("w_back")
        w_mm = sem("w_mm")
        w_turn = sem("w_turn")
        sorted_zeroed = sem("sorted_zeroed")
        a_ps = sem("a_ps")
        a_sb = sem("a_sb")
        z_ps = sem("z_ps")
        z_sb = sem("z_sb")
        z_tps = sem("z_tps")
        x1_done = sem("x1_done")
        ln_stats = sem("ln_stats")
        ln_done = sem("ln_done")
        ln_std = sem("ln_std")
        ln_rstd = sem("ln_rstd")
        ln_part_done = sem("ln_part_done")
        h2_done = sem("h2_done")
        h2_ps = sem("h2_ps")
        h2T_done = sem("h2T_done")
        route_ps = sem("route_ps")
        route_step = sem("route_step")
        top_done = sem("top_done")
        exp_top = sem("exp_top")
        rows_scaled = sem("rows_scaled")
        onehot_done = sem("onehot_done")
        place_ps = sem("place_ps")
        pos_done = sem("pos_done")
        table_done = sem("table_done")
        scattered = sem("scattered")
        gate_ps = sem("gate_ps")
        up_ps = sem("up_ps")
        silu_sb = sem("silu_sb")
        act_sb = sem("act_sb")
        down_mm = sem("down_mm")
        down_sb = sem("down_sb")
        back_ps = sem("back_ps")
        acc_done = sem("acc_done")
        xT_ps = sem("xT_ps")
        xT_sb = sem("xT_sb")
        gu_ps = sem("gu_ps")
        msilu_sb = sem("msilu_sb")
        mact_sb = sem("mact_sb")
        aT_ps = sem("aT_ps")
        aT_sb = sem("aT_sb")
        y_ps = sem("y_ps")
        y_sb = sem("y_sb")
        mix_step = sem("mix_step")
        mixed = sem("mixed")
        consts2 = sem("consts2")
        out_done = sem("out_done")
        x_loaded = [sem(f"x_loaded{b}") for b in range(BATCH)]
        bn_stats_done = [sem(f"bn_stats_done{b}") for b in range(BATCH)]
        bn_done = [sem(f"bn_done{b}") for b in range(BATCH)]
        std_done = [sem(f"std_done{b}") for b in range(BATCH)]
        rstd_done = [sem(f"rstd_done{b}") for b in range(BATCH)]
        xhat_done = [sem(f"xhat_done{b}") for b in range(BATCH)]
        turned = [sem(f"turned{b}") for b in range(BATCH)]
        hT_done = [sem(f"hT_done{b}") for b in range(BATCH)]
        q_mm = [sem(f"q_mm{b}") for b in range(BATCH)]
        k_mm = [sem(f"k_mm{b}") for b in range(BATCH)]
        pre_mm = [sem(f"pre_mm{b}") for b in range(BATCH)]
        v_mm = [sem(f"v_mm{b}") for b in range(BATCH)]
        q_out = [sem(f"q_out{b}") for b in range(BATCH)]
        k_out = [sem(f"k_out{b}") for b in range(BATCH)]
        pre_out = [sem(f"pre_out{b}") for b in range(BATCH)]
        v_out = [sem(f"v_out{b}") for b in range(BATCH)]
        q_split = [sem(f"q_split{b}") for b in range(BATCH)]
        k_split = [sem(f"k_split{b}") for b in range(BATCH)]
        k_negated = [sem(f"k_negated{b}") for b in range(BATCH)]
        pre_first = [sem(f"pre_first{b}") for b in range(BATCH)]
        pre_scaled = [sem(f"pre_scaled{b}") for b in range(BATCH)]
        q_stored = [sem(f"q_stored{b}") for b in range(BATCH)]
        pre_stored = [sem(f"pre_stored{b}") for b in range(BATCH)]
        h_stored = [sem(f"h_stored{b}") for b in range(BATCH)]
        k_ones = sem("k_ones")
        minus_k_loaded = [sem(f"minus_k_loaded{b}") for b in range(BATCH)]
        pre_loaded = [sem(f"pre_loaded{b}") for b in range(BATCH)]
        q_loaded = [[sem(f"q_loaded{b}{hf}") for hf in range(2)] for b in range(BATCH)]
        moe_loaded = [sem(f"moe_loaded{u}") for u in range(2)]
        moe_stored = [sem(f"moe_stored{u}") for u in range(2)]
        gathered = [sem(f"gathered{n}") for n in range(NG)]
        k_loaded = [sem(f"k_loaded{b}") for b in range(BATCH)]
        c_loaded = [sem(f"c_loaded{hf}") for hf in range(2)]
        block = ctx.enter_context(nc.Block())

        x_t = x.rearrange("b (t p) c -> p (b t) c", p=P)


        def pe_logits(pe, blk, j):
            t, b, i = blk
            nt, half = j // 2, j % 2
            if j == 0:
                if isinstance(i, int) and i == 0:
                    pe.wait_ge(pre_first[b], 1)
                else:
                    pe.wait_ge(pre_loaded[b], i * 16)
            else:
                pe.wait_ge(l_evac, t * 4 + j)
            pe.matmul(psum[:, MISC, :], pre_blk[:, b, nt * P:(nt + 1) * P],
                      preT[:, b, half * CH:(half + 1) * CH], start=True, stop=True).then_inc(l_done, 1)

        def act_logits(act, blk, j):
            t, b, i = blk
            nt, half = j // 2, j % 2
            act.wait_ge(l_done, t * 4 + (j + 1))
            act.activation(logits[:, b, nt, half * CH:(half + 1) * CH], psum[:, MISC, :],
                           ACT.Copy).then_inc(l_evac, 1)

        def pe_score_chunk(pe, blk, h, c, first=False):
            t, b, i = blk
            nt, half = c // 2, c % 2
            if c == 0 and h % 8 == 0:
                pe.wait_ge(q_loaded[b][h // 8], (i + 1) * 16 * Q_DMAS)
            if not (first and h == 0 and c < 2):
                pe.wait_ge(ttr_done, t * CHUNKS + (h * 4 + c - 1))
            pe.matmul(psum[:, S1B + c % 2, :], qd[0:PREV, b, h, nt * P:(nt + 1) * P],
                      kd[0:PREV, b, h, half * CH:(half + 1) * CH], start=True, stop=True).then_inc(s1_done, 1)

        def dve_max_chunk(dve, blk, h, c, chunk=None):
            t, b, i = blk
            nt, half = c // 2, c % 2
            if h == 0 and c == 0:
                dve.wait_ge(l_evac, t * 4 + 4)
            if isinstance(t, int):
                dve.wait_ge(s1_done, t * CHUNKS + h * 4 + c + 1)
            else:
                dve.wait_ge(s1_done, chunk)
                dve.reg_add(chunk, chunk, 1)
            dve.tensor_tensor_reduce(out=junk[:, c % 2, :], in0=psum[:, S1B + c % 2, :],
                                     in1=logits[:, b, nt, half * CH:(half + 1) * CH],
                                     scale=1.0, scalar=LOWEST, op0=ALU.add, op1=ALU.max,
                                     accum_out=row_max[:, b, h, nt, half:half + 1]).then_inc(ttr_done, 1)

        def dve_max_parts(dve, blk, hf, first=False):
            t, b, i = blk
            n = t * 2 + hf
            dve.wait_ge(ttr_done, t * CHUNKS + (hf + 1) * 32)
            if not (first and hf == 0):
                dve.wait_ge(cT_done, n)
            dve.tensor_reduce(neg_max[:, :, :], row_max[:, b, 8 * hf:8 * hf + 8, :, :], AX.X, ALU.max,
                              negate=True).then_inc(max_done, 1)
            dve.wait_ge(max_done, n * 2 + 1)
            dve.tensor_copy(c_parts[:, :, 0, :].rearrange("p t h -> p h t"), neg_max[:, :, :]).then_inc(max_done, 1)
            dve.wait_ge(max_done, n * 2 + 2)
            dve.tensor_tensor(c_parts[:, :, 1, :].rearrange("p t h -> p h t"), neg_max[:, :, :],
                              c_parts[:, :, 0, :].rearrange("p t h -> p h t"), ALU.subtract).then_inc(c_ready, 1)

        misc_b = psum[:, MISC, :].bitcast(BF16)

        def pe_max_rows(pe, blk, hf):
            t, b, i = blk
            pe.wait_ge(c_ready, t * 2 + (hf + 1))
            for nt in range(2):
                mm = pe.transpose(misc_b[0:16, nt * P:(nt + 1) * P],
                                  c_parts[:, nt, :, :].rearrange("p a h -> p (a h)"), ident_b[:, :])
            mm.then_inc(cT_done, 1)

        def act_max_rows(act, blk, hf, first=False):
            t, b, i = blk
            act.wait_ge(cT_done, t * 2 + (hf + 1))
            if not first:
                act.wait_ge(c_loaded[hf], t * 64)
            act.activation(cT[:, hf, :], misc_b[0:16, 0:QB], ACT.Copy).then_inc(cT_evac, 1)

        def sp_max_rows(sp, blk, hf):
            t, b, i = blk
            sp.wait_ge(cT_evac, t * 2 + (hf + 1))
            h0, n_next = 8 * hf, 8 - hf
            for part in range(2):
                sp.dma_start(qd[CROW + part:CROW + part + 1, b, h0:h0 + 8, :],
                             cT[8 * part:8 * part + 8, hf, :]).then_inc(c_loaded[hf], 16)
                sp.dma_start(qd[PREV + CROW + part:PREV + CROW + part + 1, b, h0 + 1:h0 + 1 + n_next, :],
                             cT[8 * part:8 * part + n_next, hf, :]).then_inc(c_loaded[hf], 16)

        def sp_load_pre(sp, b, at):
            sp.dma_start(pre_blk[:, b, :], pre_dram[b, :, bass.ds(at, QB)]).then_inc(pre_loaded[b], 16)

        def sp_load_q(sp, b, at, hf):
            n = bass.ds(at, QB)
            h0, h1 = 8 * hf, 8 * hf + 8
            p0 = max(h0, 1)
            sp.dma_start(qd[CROW:CROW + 2, b, h0:h1, :], zeros2[:, :].unsqueeze(1).broadcast_to([2, 8, QB])).then_inc(q_loaded[b][hf], 16)
            for slot, k in Q_RUNS:
                sp.dma_start(qd[slot * DH:(slot + k) * DH, b, h0:h1, :],
                             q_dram[b, 0:k * DH, h0:h1, n]).then_inc(q_loaded[b][hf], 16)
                sp.dma_start(qd[PREV + slot * DH:PREV + (slot + k) * DH, b, p0:h1, :],
                             q_dram[b, 0:k * DH, p0 - 1:h1 - 1, n]).then_inc(q_loaded[b][hf], 16)

        def pe_values(pe, vb, g, m):
            for j in range(GH):
                mm = pe.matmul(avp[32 * j:32 * j + DH + 1, g % 2, :], v_aug[:, vb, m, g * GH + j, :],
                               probs[:, g % 2, j, m, :], start=(m == 0), stop=(m == NT - 1),
                               skip_group_check=True)
            return mm

        def pe_norm(pe, k):
            for g in range(GROUPS):
                mm = pe.transpose(psum[:, MISC, g * P:(g + 1) * P], av_sb[:, g, k * P:(k + 1) * P], ident[:, :])
            mm.then_inc(nT_done, 1)

        def pe_block(pe, blk, first=False, last=False):
            t, b, i = blk
            for h in range(HEADS):
                g = h // GH
                for st in range(2):
                    step = 2 * h + st
                    ahead, ah = (blk, h + LEAD) if h + LEAD < HEADS else (following(blk), h + LEAD - HEADS)
                    if first and ah == 0 and st == 0:
                        pe.wait_ge(k_loaded[1], 96)
                    if ahead is blk or not last:
                        pe_score_chunk(pe, ahead, ah, 2 * st)
                    if step % 16 == 0:
                        pe.wait_ge(c_loaded[h // 8], (t + 1) * 64)
                    if not (first and h == 0):
                        pe.wait_ge(exp_done, t * STEPS + (step - 1))
                    for m in range(4 * st, 4 * st + 4):
                        keys = slice(m * P, (m + 1) * P)
                        if h == 0:
                            pe.matmul(s2p[:, m, :], preT[:, b, keys], pre_blk[:, b, :],
                                      start=(m % 2 == 0), stop=True, skip_group_check=True)
                        mm = pe.matmul(s2p[:, m, :], kd[:, b, h, keys], qd[:, b, h, :],
                                       start=False, stop=True, skip_group_check=True)
                    mm.then_inc(s2_done, 1)
                    if ahead is blk or not last:
                        pe_score_chunk(pe, ahead, ah, 2 * st + 1)
                    if not (first and g == 0):
                        if step % 8 == 0:
                            pe.wait_ge(exp_done, t * STEPS + 8 * g)
                            if first and g == 1:
                                pe.wait_ge(av_zeroed, 1)
                            else:
                                pe.wait_ge(av_evac, t * GROUPS + (g - 1))
                        mm = pe_values(pe, b if g else 1 - b, (g - 1) % GROUPS, step % 8)
                        if step % 8 == 7:
                            mm.then_inc(av_done, 1)
                    if h == 4 and st == 1 and not first:
                        pe.wait_ge(av_evac, t * GROUPS)
                        pe.wait_ge(cT_evac, t * 2 + 1)
                        pe_norm(pe, 0)
                    if h == 5 and st == 1:
                        if first:
                            pe.wait_ge(cT_evac, t * 2 + 1)
                        else:
                            pe.wait_ge(norm_done, t * 2 - 1)
                        pe_max_rows(pe, blk, 1)
                    if h == 6 and st == 1 and not first:
                        pe.wait_ge(cT_evac, t * 2 + 2)
                        pe_norm(pe, 1)
                    if h in (10, 11) and not last:
                        if h == 10 and st == 0:
                            if first:
                                pe.wait_ge(cT_evac, t * 2 + 2)
                            else:
                                pe.wait_ge(norm_done, t * 2)
                        pe_logits(pe, following(following(blk)), 2 * (h - 10) + st)
                    if h == 14 and st == 0 and not last:
                        pe.wait_ge(l_evac, t * 4 + 12)
                        pe_max_rows(pe, following(blk), 0)

        def act_values(act, blk, pg, done, first=False):
            t, b, i = blk
            act.wait_ge(av_done, done)
            if pg == 0 and not first:
                act.wait_ge(nT_done, t * 2)
            act.activation(av_sb[:, pg, :], avp[:, pg % 2, :], ACT.Copy).then_inc(av_evac, 1)

        def act_block(act, blk, first=False, last=False):
            t, b, i = blk
            for h in range(HEADS):
                g = h // GH
                for st in range(2):
                    step = 2 * h + st
                    if step % 8 == 0 and not (first and g < 2):
                        act.wait_ge(av_done, t * GROUPS + (g - 1))
                    act.wait_ge(s2_done, t * STEPS + (step + 1))
                    act.activation(probs[:, g % 2, h % GH, 4 * st:4 * st + 4, :],
                                   s2p[:, 4 * st:4 * st + 4, :], ACT.Exp).then_inc(exp_done, 1)
                    if step % 8 == 7 and not (first and g == 0):
                        act_values(act, blk, (g - 1) % GROUPS, t * GROUPS + g, first)
                    if h == 5 and st == 1:
                        act_max_rows(act, blk, 1, first)
                    if h in (10, 11) and not last:
                        act_logits(act, following(following(blk)), 2 * (h - 10) + st)
                    if h == 14 and st == 0 and not last:
                        act_max_rows(act, following(blk), 0)

        def dve_norm(dve, blk, k):
            t, b, i = blk
            m = psum[:, MISC, :].rearrange("p (h w) -> p h w", w=32)
            dve.wait_ge(nT_done, t * 2 + (k + 1))
            dve.reciprocal(recip[:, :], m[:, :, DH]).then_inc(rec_done, 1)
            dve.wait_ge(rec_done, t * 2 + (k + 1))
            dst = attn[:, b, bass.ds(i * 2 + k, 1), :].rearrange("p o (h d) -> p (o h) d", d=DH)
            dve.tensor_tensor(dst, m[:, :, 0:DH], recip[:, :].unsqueeze(2).broadcast_to([P, HEADS, DH]),
                              ALU.mult).then_inc(norm_done, 1)

        def dve_block(dve, blk, chunk=None, first=False, last=False):
            for h in range(HEADS):
                ahead, ah = (blk, h + LEAD) if h + LEAD < HEADS else (following(blk), h + LEAD - HEADS)
                if ahead is blk or not last:
                    for c in range(4):
                        dve_max_chunk(dve, ahead, ah, c, chunk)
                    if ah % 8 == 7:
                        dve_max_parts(dve, ahead, ah // 8)
                if h in (4, 6) and not first:
                    dve_norm(dve, before(blk), (h - 4) // 2)

        def sp_block(sp, blk, last=False):
            t, b, i = blk
            at = (i + 1) * QB
            if not isinstance(at, int):
                at = sp.snap(at)
            if last:
                sp_max_rows(sp, blk, 1)
                return
            sp.wait_ge(s2_done, t * STEPS + 2)
            sp_load_pre(sp, b, at)
            sp_max_rows(sp, blk, 1)
            sp.wait_ge(s2_done, t * STEPS + 16)
            sp_load_q(sp, b, at, 0)
            sp_max_rows(sp, following(blk), 0)
            sp.wait_ge(s2_done, t * STEPS + 32)
            sp_load_q(sp, b, at, 1)

        BANK_G, BANK_U, BANK_D, BANK_B = (3, 4), (5, 6), 7, 2

        def gtiles(n):
            return slice(GRP * n, GRP * n + GRP)

        def bank_tiles(bank):
            return psum[:, bank, :].rearrange("p (t c) -> p t c", c=C)

        def turn_weights(pe):
            pe.wait_ge(w_back, 16 * 7)
            pe.wait_ge(ttr_done, BLOCKS * CHUNKS)
            for w in range(3):
                if w == 2:
                    pe.wait_ge(w_turn, 1)
                for k in range(4):
                    mm = pe.transpose(psum[:, 4 + w % 2, k * P:(k + 1) * P], w_raw[:, w, k, :], ident[:, :])
                mm.then_inc(w_mm, 1)
            pe.wait_ge(w_turn, 2)
            pe.transpose(psum[:, 5, 0:EXPERTS], r_raw, ident[0:EXPERTS, 0:EXPERTS]).then_inc(w_mm, 1)
            pe.wait_ge(w_turn, 4)
            pe.wait_ge(scb_done, BATCH)
            for b in range(BATCH):
                pe.matmul(psum[:, 4 + b, 0:3 * C], silu_cb[:, b, :], wmod_rows, start=True, stop=True).then_inc(mod_rows_mm, 1)

        def copy_weights(dve):
            dve.wait_ge(s2_done, (BLOCKS - 1) * STEPS + 2)
            for w, (dst, src) in enumerate(((w_gT, psum[:, 4, :]), (w_uT, psum[:, 5, :]),
                                            (preT[:, 1, 0:SF], psum[:, 4, :]), (w_rT, psum[:, 5, 0:EXPERTS]))):
                dve.wait_ge(w_mm, w + 1)
                dve.tensor_copy(dst, src).then_inc(w_turn, 1)
            for b in range(BATCH):
                dve.tensor_copy(silu_cb[:, b, :], silu_c[:, b:b + 1].broadcast_to([P, P])).then_inc(scb_done, 1)
            dve.wait_ge(ttr_done, BLOCKS * CHUNKS)
            for b in range(BATCH):
                dve.wait_ge(mod_rows_mm, b + 1)
                src = psum[:, 4 + b, 0:3 * C].rearrange("p (k c) -> p k c", k=3)
                dve.tensor_copy(mod_rows[:, b, 0, :], src[:, 0, :]).then_inc(mod_rows_done, 1)
                dve.tensor_scalar(mod_rows[:, b, 1, :], src[:, 1, :], 1.0, None, ALU.add).then_inc(mod_rows_done, 1)
                if b:
                    dve.wait_ge(mod_rows_done, 3)
                dve.tensor_scalar(gate_step, src[:, 2, :], 0.0, 2.0, ALU.is_ge, ALU.mult).then_inc(mod_steps, 1)
                dve.wait_ge(mod_steps, 3 * b + 1)
                dve.tensor_scalar(gate_sign, gate_step, -1.0, None, ALU.add).then_inc(mod_steps, 1)
                dve.scalar_tensor_tensor(out=gate_size, in0=gate_step, scalar=-1.0, in1=src[:, 2, :],
                                         op0=ALU.add, op1=ALU.mult).then_inc(mod_steps, 1)
                dve.wait_ge(mod_steps, 3 * b + 3)
                dve.scalar_tensor_tensor(out=mod_rows[:, b, 2, :], in0=gate_size, scalar=0.25, in1=gate_sign,
                                         op0=ALU.max, op1=ALU.mult).then_inc(mod_rows_done, 1)

        def ffn_sync(sp):
            sp.wait_ge(s2_done, (BLOCKS - 1) * STEPS)
            sp.dma_start(w_raw[:, 0, :, :], shared_gate_w.rearrange("(k p) c -> p k c", p=P)).then_inc(w_back, 16)
            sp.dma_start(w_raw[:, 1, :, :], shared_up_w.rearrange("(k p) c -> p k c", p=P)).then_inc(w_back, 16)
            sp.dma_start(w_raw[:, 2, :, :], shared_down_w.rearrange("p (k c) -> p k c", c=P)).then_inc(w_back, 16)
            sp.dma_start(r_raw, router_w).then_inc(w_back, 16)
            sp.dma_start(wmod_rows, wmod[:, 3 * C:6 * C]).then_inc(w_back, 16)
            sp.dma_start(w_gu.rearrange("p (e f) -> p e f", e=EXPERTS),
                         gate_up_w.rearrange("e h f -> h e f")).then_inc(w_back, 16)
            sp.dma_start(w_dn.rearrange("p (e f) -> p e f", e=EXPERTS),
                         down_w.rearrange("e f h -> f e h")).then_inc(w_back, 16)
            sp.wait_ge(c_ready, 2 * BLOCKS)
            for b in range(BATCH):
                sp.dma_start(x_back[:, b, :, :], tokens[:, b * NT:(b + 1) * NT, :]).then_inc(x_back_loaded, 16)
                sp.dma_start(h_back[:, b, :], h_dram[:, b * SEQ:(b + 1) * SEQ]).then_inc(h_back_loaded, 16)
            sp.wait_ge(scattered, 16 * NTA)

            def load(c, u):
                src = sorted_dram[bass.ds(c * (GRP * P), GRP * P), :].rearrange("(t p) c -> p t c", p=P)
                sp.dma_start(moe_x[:, u, :, :], src).then_inc(moe_loaded[u], 16)

            def store(c, u):
                dst = expert_dram[bass.ds(c * (GRP * P), GRP * P), :].rearrange("(t p) c -> p t c", p=P)
                sp.wait_ge(y_sb, c + 1)
                sp.dma_start(dst, moe_y[:, u, :, :]).then_inc(moe_stored[u], 16)

            load(0, 0)
            load(1, 1)

            def step(c, u, begin=False, left=3):
                if left > 2:
                    sp.wait_ge(xT_ps, c + 1)
                    load(c + 2, u)
                if not begin:
                    store(c - 1, 1 - u)

            moe_loop(sp, step)
            store(MOE_CHUNKS - 1, 1)
            for n in range(NG):
                sp.wait_ge(mixed, n + 1)
                sp.dma_start(out_tokens[:, gtiles(n), :], acc[:, gtiles(n), :]).then_inc(out_done, 16)
            sp.wait_ge(out_done, 16 * NG)

        def ffn_pool(pool):
            pool.memset(zero_rows[:, :], 0.0).then_inc(consts2, 1)
            pool.wait_ge(consts2, 1)
            for k in range(MOE_TILES // GRP):
                pool.dma_start(sorted_dram[k * GRP * P:(k + 1) * GRP * P, :].rearrange("(t p) c -> p t c", p=P),
                               zero_rows[:, :].unsqueeze(1).broadcast_to([P, GRP, C])).then_inc(sorted_zeroed, 16)
            pool.wait_ge(av_done, BLOCKS * GROUPS)
            pool.memset(upper32, 1.0).then_inc(consts2, 1)
            pool.wait_ge(consts2, 2)
            pool.affine_select(out=upper32, in_=upper32, compare_op=ALU.is_gt, fill=0.0, base=0,
                               pattern=[[1, P]], channel_multiplier=-1).then_inc(consts2, 1)
            pool.wait_ge(consts2, 3)
            pool.tensor_copy(upper_b, upper32).then_inc(consts2, 1)
            pool.memset(ones_b, 1.0).then_inc(consts2, 1)
            pool.iota(weight_e.bitcast(I32), pattern=[[-1, EXPERTS]], base=EXPERTS,
                      channel_multiplier=0).then_inc(consts2, 1)
            pool.iota(tab_j.bitcast(I32), pattern=[[1, MOE_TILES]], base=0, channel_multiplier=0).then_inc(consts2, 1)
            pool.wait_ge(sorted_zeroed, 16 * (MOE_TILES // GRP))
            pool.wait_ge(pos_done, 1)
            for t in range(NTA):
                pool.wait_ge(rows_scaled, t // GRP + 1)
                pool.indirect_dma_start(out=sorted_dram, out_offset=bass.IndirectOffsetOnAxis(ap=pos[:, t:t + 1], axis=0),
                                        in_=rows[:, t, :], in_offset=None).then_inc(scattered, 16)
            for u in range(2):
                pool.wait_ge(moe_stored[u], 16 * (MOE_CHUNKS // 2))
            for t in range(NTA):
                pool.indirect_dma_start(out=got[:, t, :], out_offset=None, in_=expert_dram,
                                        in_offset=bass.IndirectOffsetOnAxis(ap=pos[:, t:t + 1], axis=0)
                                        ).then_inc(gathered[t // GRP], 16)

        def pe_shared(pe, n, steps=range(5)):
            cols = h2T[:, n * CH:(n + 1) * CH]
            for k in steps:
                if k < 4:
                    u, at = k % 2, 4 * n + k
                    if at >= 2:
                        pe.wait_ge(act_sb, at - 1)
                    pe.matmul(psum[:, BANK_G[u], :], w_gT[:, k * P:(k + 1) * P], cols, start=True,
                              stop=True).then_inc(gate_ps, 1)
                    pe.matmul(psum[:, BANK_U[u], :], w_uT[:, k * P:(k + 1) * P], cols, start=True,
                              stop=True).then_inc(up_ps, 1)
                if k:
                    if k == 1 and n:
                        pe.wait_ge(down_sb, n)
                    pe.wait_ge(act_sb, 4 * n + k)
                    pe.matmul(psum[:, BANK_D, :], w_dT[:, k - 1, :], ff_act[:, (k - 1) % 2, :],
                              start=(k == 1), stop=(k == 4)).then_inc(down_mm, 1)

        def pe_shared_back(pe, n):
            pe.wait_ge(down_sb, n + 1)
            if n:
                pe.wait_ge(acc_done, n)
            for k in range(GRP):
                mm = pe.transpose(psum[:, BANK_B, k * P:(k + 1) * P], ff_out[:, n % 2, k * P:(k + 1) * P], ident[:, :])
            mm.then_inc(back_ps, 1)

        def act_shared(act, n):
            for k in range(4):
                at = 4 * n + k
                if at >= 2:
                    act.wait_ge(act_sb, at - 1)
                act.wait_ge(gate_ps, at + 1)
                act.activation(ff_silu[:, k % 2, :], psum[:, BANK_G[k % 2], :], ACT.Silu).then_inc(silu_sb, 1)
            act.wait_ge(down_mm, 4 * n + 4)
            if n >= 2:
                act.wait_ge(back_ps, n - 1)
            act.activation(ff_out[:, n % 2, :], psum[:, BANK_D, :], ACT.Identity,
                           scale=mod_cols[:, 3, n // 2:n // 2 + 1]).then_inc(down_sb, 1)

        def dve_shared(dve, n, steps=range(4)):
            for k in steps:
                at = 4 * n + k
                if at >= 2:
                    dve.wait_ge(down_mm, at - 1)
                dve.wait_ge(silu_sb, at + 1)
                dve.wait_ge(up_ps, at + 1)
                dve.tensor_tensor(ff_act[:, k % 2, :], psum[:, BANK_U[k % 2], :], ff_silu[:, k % 2, :],
                                  ALU.mult).then_inc(act_sb, 1)

        def dve_shared_back(dve, n):
            dve.wait_ge(back_ps, n + 1)
            dve.tensor_tensor(acc[:, gtiles(n), :], bank_tiles(BANK_B), x1[:, gtiles(n), :],
                              ALU.add).then_inc(acc_done, 1)

        GU_BANKS, BANK_X, BANK_A, BANK_Y = (3, 5), 0, 1, 7

        def gate_up_view(u):
            return psum[:, GU_BANKS[u]:GU_BANKS[u] + 2, :].rearrange("p b (t f) -> p (b t) f", f=2 * F)

        def pe_tile_experts(pe, c):
            loads, experts = nc.values_load_multi_w_load_instructions(
                tile_expert[0:1, bass.ds(c * GRP, GRP)], engines=(mybir.EngineType.PE,), min_val=0,
                max_val=EXPERTS - 1)
            return experts

        def pe_moe_turn(pe, c, u):
            pe.wait_ge(moe_loaded[u], (c - u) * 8 + 16)
            for k in range(GRP):
                mm = pe.transpose(psum[:, BANK_X, k * P:(k + 1) * P], moe_x[:, u, k, :], ident[:, :])
            mm.then_inc(xT_ps, 1)

        def pe_moe_up(pe, c, u, begin=False):
            experts = pe_tile_experts(pe, c)
            if not begin:
                pe.wait_ge(mact_sb, c - 1)
            pe.wait_ge(xT_sb, c + 1)
            for k, e in enumerate(experts):
                mm = pe.matmul(gate_up_view(u)[:, k, :], moe_xT[:, k, :],
                               w_gu[:, bass.ds(e * (2 * F), 2 * F)], start=True, stop=True)
            mm.then_inc(gu_ps, 1)

        def pe_moe_turn_act(pe, c, begin=False):
            pe.wait_ge(mact_sb, c + 1)
            if not begin:
                pe.wait_ge(aT_sb, c)
            for k in range(GRP):
                mm = pe.transpose(psum[:, BANK_A, k * P:(k + 1) * P], moe_act[:, k, :], ident[:, :])
            mm.then_inc(aT_ps, 1)

        def pe_moe_down(pe, c, begin=False):
            experts = pe_tile_experts(pe, c)
            if not begin:
                pe.wait_ge(y_sb, c)
            pe.wait_ge(aT_sb, c + 1)
            for k, e in enumerate(experts):
                mm = pe.matmul(psum[:, BANK_Y, k * P:(k + 1) * P], moe_aT[:, k, :], w_dn[:, bass.ds(e * C, C)],
                               start=True, stop=True)
            mm.then_inc(y_ps, 1)

        def act_moe_x(act, c):
            act.wait_ge(xT_ps, c + 1)
            act.activation(moe_xT, bank_tiles(BANK_X), ACT.Copy).then_inc(xT_sb, 1)

        def act_moe_silu(act, c, u, begin=False):
            if not begin:
                act.wait_ge(mact_sb, c)
            act.wait_ge(gu_ps, c + 1)
            act.activation(moe_silu, gate_up_view(u)[:, :, 0:F], ACT.Silu).then_inc(msilu_sb, 1)

        def act_moe_y(act, c, u, begin=False):
            act.wait_ge(y_ps, c + 1)
            if not begin:
                act.wait_ge(moe_stored[u], (c - u) * 8)
            act.activation(moe_y[:, u, :, :], bank_tiles(BANK_Y), ACT.Copy).then_inc(y_sb, 1)

        def dve_moe_act(dve, c, u, begin=False):
            if not begin:
                dve.wait_ge(aT_ps, c)
            dve.wait_ge(msilu_sb, c + 1)
            dve.tensor_tensor(moe_act, gate_up_view(u)[:, :, F:2 * F], moe_silu, ALU.mult).then_inc(mact_sb, 1)

        def dve_moe_turned(dve, c, begin=False):
            if not begin:
                dve.wait_ge(y_ps, c)
            dve.wait_ge(aT_ps, c + 1)
            dve.tensor_copy(moe_aT, bank_tiles(BANK_A)).then_inc(aT_sb, 1)

        def moe_loop(eng, step):
            step(0, 0, begin=True)
            step(1, 1)
            with eng.Fori(1, MOE_CHUNKS // 2 - 1) as k:
                for u in range(2):
                    step(k * 2 + u, u)
            step(MOE_CHUNKS - 2, 0, left=2)
            step(MOE_CHUNKS - 1, 1, left=1)

        def ffn_pe(pe):
            def turn_attn(n):
                if n >= 2:
                    pe.wait_ge(a_sb, n - 1)
                for k in range(GRP):
                    t = GRP * n + k
                    mm = pe.transpose(psum[:, n % 2, k * P:(k + 1) * P], attn[:, t // NT, t % NT, :], ident[:, :])
                mm.then_inc(a_ps, 1)

            def project(n):
                pe.wait_ge(a_sb, n + 1)
                if n >= 2:
                    pe.wait_ge(z_sb, n - 1)
                pe.matmul(psum[:, 2 + n % 2, :], weights[:, 4, :], aT[:, n % 2, :], start=True,
                          stop=True).then_inc(z_ps, 1)

            def turn_back(n):
                pe.wait_ge(z_sb, n + 1)
                if n >= 2:
                    pe.wait_ge(x1_done, n - 1)
                for k in range(GRP):
                    mm = pe.transpose(psum[:, 4 + n % 2, k * P:(k + 1) * P], zT[:, n % 2, k * P:(k + 1) * P], ident[:, :])
                mm.then_inc(z_tps, 1)

            def turn_h2(n):
                pe.wait_ge(h2_done, GRP * (n + 1))
                if n >= 2:
                    pe.wait_ge(h2T_done, n - 1)
                for k in range(GRP):
                    mm = pe.transpose(psum[:, 6 + n % 2, k * P:(k + 1) * P], h2[:, GRP * n + k, :], ident[:, :])
                mm.then_inc(h2_ps, 1)

            def router(n):
                pe.wait_ge(h2T_done, n + 1)
                for k in range(GRP):
                    t = GRP * n + k
                    mm = pe.matmul(psum[:, 0, t * EXPERTS:(t + 1) * EXPERTS], h2T[:, t * P:(t + 1) * P], w_rT,
                                   start=True, stop=True)
                mm.then_inc(route_ps, 1)

            pe.wait_ge(norm_done, NTA)
            pe.wait_ge(mod_rows_done, 3 * BATCH)
            turn_attn(0); turn_attn(1); project(0); project(1)
            turn_back(0); turn_attn(2); turn_back(1); turn_attn(3)
            project(2); project(3); turn_back(2); turn_back(3)
            turn_h2(0); turn_h2(1)
            pe.wait_ge(a_sb, NG)
            router(0); turn_h2(2); router(1); turn_h2(3); router(2); router(3)
            pe.wait_ge(x1_done, NG)
            pe.wait_ge(z_sb, NG)
            pe_shared(pe, 0, range(0, 2))
            pe.wait_ge(onehot_done, 1)
            pe.wait_ge(consts2, 5)
            pe.matmul(psum[:, 1, 0:256], upper_b, onehot_b.rearrange("p t e -> p (t e)"), start=True, stop=False,
                      skip_group_check=True)
            for k in range(1, NTA):
                mm = pe.matmul(psum[:, 1, k * EXPERTS:256], ones_b,
                               onehot_b[:, 0:NTA - k, :].rearrange("p t e -> p (t e)"), start=False,
                               stop=(k == NTA - 1), skip_group_check=True)
            mm.then_inc(place_ps, 1)
            for k in range(NTA):
                mm = pe.matmul(psum[:, 0, 256:256 + EXPERTS], ones_b, onehot_b[:, k, :], start=(k == 0),
                               stop=(k == NTA - 1), skip_group_check=True)
            mm.then_inc(place_ps, 1)
            pe_shared(pe, 0, range(2, 5))
            pe_shared_back(pe, 0)
            for n in (1, 2):
                pe_shared(pe, n)
                pe_shared_back(pe, n)
            pe.wait_ge(pos_done, 1)
            pe.wait_ge(table_done, 1)
            pe.wait_ge(act_sb, 12)
            pe.wait_ge(down_sb, 3)
            pe_moe_turn(pe, 0, 0)
            pe_moe_up(pe, 0, 0, begin=True)
            pe.wait_ge(xT_sb, 1)
            pe_moe_turn(pe, 1, 1)

            def step(c, u, begin=False, left=3):
                if left > 1:
                    pe_moe_up(pe, c + 1, 1 - u, begin=begin)
                pe_moe_turn_act(pe, c, begin=begin)
                if left > 2:
                    pe.wait_ge(xT_sb, c + 2)
                    pe_moe_turn(pe, c + 2, u)
                if not begin:
                    pe_moe_down(pe, c - 1, begin=isinstance(c, int) and c == 1)

            moe_loop(pe, step)
            pe_moe_down(pe, MOE_CHUNKS - 1)
            pe.wait_ge(y_sb, MOE_CHUNKS)
            pe_shared(pe, 3)
            pe_shared_back(pe, 3)

        def ffn_act(act):
            for n in range(NG):
                act.wait_ge(a_ps, n + 1)
                if n >= 2:
                    act.wait_ge(z_ps, n - 1)
                act.activation(aT[:, n % 2, :], psum[:, n % 2, :], ACT.Copy).then_inc(a_sb, 1)
            for n in range(NG):
                act.wait_ge(ln_done, GRP * (n + 1))
                act.activation(std[:, gtiles(n)], mv[:, gtiles(n), 1], ACT.Sqrt, bias=small[:, 0:1]).then_inc(ln_std, 1)
            for n in range(NG):
                act.wait_ge(h2_ps, n + 1)
                act.activation(h2T[:, n * CH:(n + 1) * CH], psum[:, 6 + n % 2, :], ACT.Copy).then_inc(h2T_done, 1)
            act.wait_ge(top_done, 1)
            act.activation(tok[:, 1, :], tok[:, 0, :], ACT.Exp, scale=-1.0).then_inc(exp_top, 1)
            for n in range(3):
                act_shared(act, n)
            act_moe_x(act, 0)
            act_moe_silu(act, 0, 0, begin=True)
            act_moe_x(act, 1)

            def step(c, u, begin=False, left=3):
                if left > 1:
                    act_moe_silu(act, c + 1, 1 - u)
                if left > 2:
                    act_moe_x(act, c + 2)
                if not begin:
                    act_moe_y(act, c - 1, 1 - u, begin=isinstance(c, int) and c <= 2)

            moe_loop(act, step)
            act_moe_y(act, MOE_CHUNKS - 1, 1)
            act_shared(act, 3)

        def ffn_dve(dve):
            def gate_out(n):
                b = n // 2
                dve.wait_ge(z_ps, n + 1)
                if n == 0:
                    dve.wait_ge(h_back_loaded, 32)
                    dve.wait_ge(x_back_loaded, 32)
                    dve.wait_ge(av_done, BLOCKS * GROUPS)
                dve.scalar_tensor_tensor(out=zpart[:, n % 2, :], in0=psum[:, 2 + n % 2, :], scalar=small[:, 3:4],
                                         in1=h_back[:, b, (n % 2) * CH:(n % 2 + 1) * CH], op0=ALU.add,
                                         op1=ALU.add).then_inc(z_part, 1)
                dve.wait_ge(z_part, n + 1)
                if n >= 2:
                    dve.wait_ge(z_tps, n - 1)
                dve.tensor_scalar(zT[:, n % 2, :], zpart[:, n % 2, :], mod_cols[:, 2, b:b + 1], None,
                                  ALU.mult).then_inc(z_sb, 1)

            def residual(n):
                b = n // 2
                dve.wait_ge(z_tps, n + 1)
                dve.tensor_tensor(x1[:, gtiles(n), :], bank_tiles(4 + n % 2),
                                  x_back[:, b, GRP * (n % 2):GRP * (n % 2) + GRP, :], ALU.add).then_inc(x1_done, 1)
                dve.wait_ge(x1_done, n + 1)
                for k in range(GRP):
                    dve.bn_stats(stats[:, GRP * n + k, :], x1[:, GRP * n + k, :]).then_inc(ln_stats, 1)
                for k in range(GRP):
                    dve.wait_ge(ln_stats, GRP * n + k + 1)
                    dve.bn_aggr(mv[:, GRP * n + k, :], stats[:, GRP * n + k, :]).then_inc(ln_done, 1)

            def norm2(n):
                b = n // 2
                dve.wait_ge(ln_std, n + 1)
                dve.reciprocal(rstd[:, gtiles(n)], std[:, gtiles(n)]).then_inc(ln_rstd, 1)
                dve.wait_ge(ln_rstd, n + 1)
                for k in range(GRP):
                    t = GRP * n + k
                    if t >= 2:
                        dve.wait_ge(h2_done, t - 1)
                    dve.scalar_tensor_tensor(out=ln_part[:, t % 2, :], in0=x1[:, t, :], scalar=mv[:, t, 0:1],
                                             in1=mod_rows[:, b, 1, :], op0=ALU.subtract,
                                             op1=ALU.mult).then_inc(ln_part_done, 1)
                    dve.wait_ge(ln_part_done, t + 1)
                    dve.scalar_tensor_tensor(out=h2[:, t, :], in0=ln_part[:, t % 2, :], scalar=rstd[:, t:t + 1],
                                             in1=mod_rows[:, b, 0, :], op0=ALU.mult,
                                             op1=ALU.add).then_inc(h2_done, 1)

            gate_out(0); gate_out(1); residual(0); residual(1)
            gate_out(2); norm2(0); gate_out(3); residual(2); norm2(1); residual(3); norm2(2); norm2(3)

            scores = psum[:, 0, 0:256].rearrange("p (t e) -> p t e", e=EXPERTS)
            logit, is_top, ranked, onehot, place = (route[:, k, :, :] for k in range(5))
            wide = [P, NTA, EXPERTS]

            def bc(v):
                return v.unsqueeze(2).broadcast_to(wide)

            r = [0]

            def routed(ins):
                r[0] += 1
                ins.then_inc(route_step, 1)
                dve.wait_ge(route_step, r[0])

            dve.wait_ge(route_ps, NG)
            dve.wait_ge(consts2, 7)
            routed(dve.tensor_copy(weight_e, weight_e.bitcast(I32)))
            routed(dve.tensor_copy(logit, scores))
            dve.tensor_reduce(tok[:, 0, :], logit, AX.X, ALU.max).then_inc(top_done, 1)
            dve.wait_ge(top_done, 1)
            routed(dve.tensor_tensor(is_top, logit, bc(tok[:, 0, :]), ALU.is_ge))
            routed(dve.tensor_tensor(ranked, is_top, weight_e.unsqueeze(1).broadcast_to(wide), ALU.mult))
            routed(dve.tensor_reduce(tok[:, 3, :], ranked, AX.X, ALU.max))
            routed(dve.tensor_tensor(onehot, ranked, bc(tok[:, 3, :]), ALU.is_equal))
            dve.tensor_copy(onehot_b, onehot).then_inc(onehot_done, 1)
            dve_shared(dve, 0, range(0, 2))
            dve.wait_ge(exp_top, 1)
            routed(dve.tensor_scalar(tok[:, 2, :], tok[:, 1, :], 1.0, None, ALU.add))
            routed(dve.reciprocal(tok[:, 4, :], tok[:, 2, :]))
            for n in range(NG):
                dve.tensor_tensor(rows[:, gtiles(n), :], h2[:, gtiles(n), :],
                                  tok[:, 4, gtiles(n)].unsqueeze(2).broadcast_to([P, GRP, C]),
                                  ALU.mult).then_inc(rows_scaled, 1)
            dve.wait_ge(place_ps, 2)
            routed(dve.tensor_scalar(e_int[:, 0, :], psum[:, 0, 256:256 + EXPERTS], float(P - 1), None, ALU.add))
            routed(dve.tensor_scalar(e_int[:, 1, :], e_int[:, 0, :], 7, None, ALU.arith_shift_right))
            routed(dve.tensor_copy(per_e[:, 0, :], e_int[:, 1, :]))
            routed(dve.memset(per_e[:, 1, :], 1.0))
            routed(dve.tensor_tensor_scan(per_e[:, 2, :], per_e[:, 1, :], per_e[:, 0, :], 0.0, ALU.mult, ALU.add))
            routed(dve.tensor_tensor(per_e[:, 3, :], per_e[:, 2, :], per_e[:, 0, :], ALU.subtract))
            routed(dve.tensor_scalar(per_e[:, 4, :], per_e[:, 3, :], float(P), None, ALU.mult))
            routed(dve.tensor_tensor(place, psum[:, 1, 0:256].rearrange("p (t e) -> p t e", e=EXPERTS),
                                     per_e[:, 4, :].unsqueeze(1).broadcast_to(wide), ALU.add))
            routed(dve.tensor_tensor(ranked, place, onehot, ALU.mult))
            routed(dve.tensor_reduce(tok[:, 5, :], ranked, AX.X, ALU.add))
            dve.tensor_copy(pos[:, :], tok[:, 5, :]).then_inc(pos_done, 1)
            routed(dve.tensor_copy(tab_jf, tab_j.bitcast(I32)))
            routed(dve.tensor_tensor(tab[:, 0:MOE_TILES, :], per_e[0:1, 2, :].unsqueeze(1).broadcast_to([1, MOE_TILES, EXPERTS]),
                                     tab_jf.unsqueeze(2).broadcast_to([1, MOE_TILES, EXPERTS]), ALU.is_le))
            routed(dve.tensor_reduce(tab_e, tab[:, 0:MOE_TILES, :], AX.X, ALU.add))
            dve.tensor_scalar(tile_expert[:, :], tab_e, float(EXPERTS - 1), None, ALU.min).then_inc(table_done, 1)
            dve_shared(dve, 0, range(2, 4))
            dve_shared_back(dve, 0)
            for n in (1, 2):
                dve_shared(dve, n)
                dve_shared_back(dve, n)
            dve_moe_act(dve, 0, 0, begin=True)

            def step(c, u, begin=False, left=3):
                if left > 1:
                    dve_moe_act(dve, c + 1, 1 - u)
                dve_moe_turned(dve, c, begin=begin)

            moe_loop(dve, step)
            dve_shared(dve, 3)
            dve_shared_back(dve, 3)
            for n in range(NG):
                b = n // 2
                dve.wait_ge(gathered[n], 16 * GRP)
                dve.tensor_tensor(got[:, gtiles(n), :], got[:, gtiles(n), :],
                                  mod_rows[:, b, 2, :].unsqueeze(1).broadcast_to([P, GRP, C]),
                                  ALU.mult).then_inc(mix_step, 1)
                dve.wait_ge(mix_step, n + 1)
                dve.wait_ge(acc_done, n + 1)
                dve.tensor_tensor(acc[:, gtiles(n), :], acc[:, gtiles(n), :], got[:, gtiles(n), :],
                                  ALU.add).then_inc(mixed, 1)

        out_tokens = out.rearrange("b (t p) c -> p (b t) c", p=P)
        tokens = x.rearrange("b (t p) c -> p (b t) c", p=P)

        def split_of(b, w):
            return (k_split if w else q_split)[b]

        def split_part(eng, b, w, part):
            src = rest[:, w, :] if part else qk32[:, w, :]
            if part:
                eng.wait_ge(split_of(b, w), 2)
            else:
                eng.wait_ge((k_out if w else q_out)[b], 2)
            if eng is nc.scalar:
                ins = eng.activation(parts[b][w][:, part, :], src, ACT.Copy)
            else:
                ins = eng.tensor_copy(parts[b][w][:, part, :], src)
            ins.then_inc(split_of(b, w), 1)

        def split_rest(eng, b, w, part):
            eng.wait_ge(split_of(b, w), 2 * part + 1)
            src, dst = (rest, parts[b][w][:, 2, :]) if part else (qk32, rest[:, w, :])
            eng.tensor_tensor(dst, src[:, w, :], parts[b][w][:, part, :], ALU.subtract).then_inc(split_of(b, w), 1)

        @block.sync
        def _(sp):
            for b in range(BATCH):
                sp.dma_start(xs[:, b * NT:(b + 1) * NT, :], tokens[:, b * NT:(b + 1) * NT, :]).then_inc(x_loaded[b], 16)
            for b in range(BATCH):
                def store_q(part):
                    sp.dma_start(q_dram[b, part * DH:(part + 1) * DH, :, 0:SEQ].rearrange("d h n -> (d h) n"),
                                 parts[b][0][:, part, :]).then_inc(q_stored[b], 16)

                def load_k(part):
                    for slot in range(6):
                        if K_PART[slot] == part:
                            sp.dma_start(kd[slot * DH:(slot + 1) * DH, b, :, :],
                                         parts[b][1][:, part, :]).then_inc(k_loaded[b], 16)

                if b:
                    sp.wait_ge(consts, 8)
                else:
                    sp.wait_ge(k_ones, 1)
                for part, step in enumerate((1, 3, 4)):
                    sp.wait_ge(k_split[b], step)
                    load_k(part)
                    sp.wait_ge(q_split[b], step)
                    store_q(part)
                sp.wait_ge(q_stored[b], 48)
                if b:
                    sp.wait_ge(consts, 12)
                else:
                    sp.wait_ge(consts, 4)
                for hf in range(2):
                    sp_load_q(sp, b, 0, hf)
                sp.wait_ge(k_negated[b], 1)
                if b:
                    sp.wait_ge(consts, 9)
                else:
                    sp.wait_ge(consts, 6)
                for slot, part in enumerate(K_PART):
                    first = (b * HEADS + 1) * SEQ
                    sp.dma_start(kd_flat[PREV + slot * DH:PREV + (slot + 1) * DH, first:first + HEADS * SEQ],
                                 parts[b][2][:, part, :]).then_inc(minus_k_loaded[b], 16)
                sp.wait_ge(pre_scaled[b], 1)
                sp.dma_start(pre_dram[b, :, 0:SEQ], preS).then_inc(pre_stored[b], 16)
                sp.dma_start(h_dram[:, b * SEQ:(b + 1) * SEQ], hT[:, b, :]).then_inc(h_stored[b], 16)
            sp.wait_ge(store_pad, 64)
            for b in range(BATCH):
                sp.wait_ge(pre_stored[b], 16)
            sp_max_rows(sp, (0, 0, 0), 0)
            sp_block(sp, (0, 0, 0))
            with sp.Fori(0, LOOPS) as k:
                sp_block(sp, (k * 2 + 1, 1, k))
                sp_block(sp, (k * 2 + 2, 0, k + 1))
            sp_block(sp, (BLOCKS - 1, 1, NT // 2 - 1), last=True)
            ffn_sync(sp)
            for hf in range(2):
                sp.wait_ge(q_loaded[0][hf], (NT // 2 + 1) * 16 * Q_DMAS)

        @block.gpsimd
        def _(pool):
            pool.memset(small[:, 0:1], EPS).then_inc(consts, 1)
            pool.memset(ident[:, :], 0.0).then_inc(ident_ready, 1)
            pool.wait_ge(ident_ready, 1)
            pool.affine_select(out=ident[:, :], in_=ident[:, :], compare_op=ALU.not_equal, fill=1.0, base=0,
                               pattern=[[-1, P]], channel_multiplier=1).then_inc(ident_ready, 1)
            pool.wait_ge(ident_ready, 2)
            pool.tensor_copy(ident_b[:, :], ident[:, :]).then_inc(ident_ready, 1)
            pool.wait_ge(ld_w, 128)
            pool.tensor_copy(w_dh.rearrange("p w (d h) -> p w d h", d=DH),
                             weights[:, 0:2, :].rearrange("p w (h d) -> p w d h", d=DH)).then_inc(w_turned, 1)
            pool.wait_ge(w_turned, 1)
            fills = ((zeros2[:, :], 0.0),
                     (qd[32:64, 0, :, :].bitcast(F32), 0.0),
                     (qd[64:128, 0, :, :].bitcast(F32), 0.0),
                     (v_aug[:, :, :, :, :], 1.0),
                     (kd[96:128, 0, :, :].bitcast(F32), MINUS_ONE_PAIR),
                     (kd[64:128, 0, 0, :].bitcast(F32), 0.0),
                     (kd[32:64, 1, :, :].bitcast(F32), ONE_PAIR),
                     (kd[96:128, 1, 1:, :].bitcast(F32), MINUS_ONE_PAIR),
                     (kd[64:128, 1, 0, :].bitcast(F32), 0.0),
                     (qd[32:64, 1, :, :].bitcast(F32), 0.0),
                     (qd[64:128, 1, :, :].bitcast(F32), 0.0))
            for n, (tile, value) in enumerate(fills):
                pool.wait_ge(consts, n + 1)
                if n == 8:
                    pool.wait_ge(minus_k_loaded[0], 96)
                pool.memset(tile, value).then_inc(consts, 1)
            pool.wait_ge(consts, 12)
            pool.memset(attn[:, 0, 0:3, :], 0.0).then_inc(pad_zeroed, 1)
            pool.wait_ge(pad_zeroed, 1)
            zeros = attn[:, 0, 0:3, :].rearrange("p t c -> p (t c)")
            pool.dma_start(pre_dram[0, :, SEQ:PAD], zeros[:, 0:QB]).then_inc(store_pad, 16)
            for part in range(3):
                pool.dma_start(q_dram[0, part * DH:(part + 1) * DH, :, SEQ:PAD].rearrange("d h n -> (d h) n"),
                               zeros.bitcast(BF16)[:, part * QB:(part + 1) * QB]).then_inc(store_pad, 16)
            for part in range(2):
                for w in (1, 0):
                    split_rest(pool, 1, w, part)
            pool.wait_ge(k_split[1], 4)
            pool.tensor_scalar(parts[1][2], parts[1][1], -1.0, None, ALU.mult).then_inc(k_negated[1], 1)
            ffn_pool(pool)

        @block.tensor
        def _(pe):
            def turn(b):
                for n, bank in enumerate(TURN_BANKS[b]):
                    pe.wait_ge(xhat_done[b], 4 * n + 4)
                    for k in range(4):
                        mm = pe.transpose(psum[:, bank, k * P:(k + 1) * P], xhat[:, b * NT + 4 * n + k, :], ident[:, :])
                    mm.then_inc(turned[b], 1)

            def project_cols(b, banks, w, done, free=()):
                for half in range(2):
                    if free:
                        pe.wait_ge(*free[half])
                    pe.wait_ge(hT_done[b], half + 1)
                    pe.matmul(psum[:, banks[b][half], :], w, hT[:, b, half * CH:(half + 1) * CH], start=True,
                              stop=True).then_inc(done[b], 1)

            def project_values(b, free):
                for half in range(2):
                    pe.wait_ge(free, half + 1)
                    for k in range(4):
                        at = half * CH + k * P
                        mm = pe.matmul(psum[:, V_BANKS[b][half], k * P:(k + 1) * P], hT[:, b, at:at + P],
                                       weights[:, 2, :], start=True, stop=True)
                    mm.then_inc(v_mm[b], 1)

            pe.wait_ge(ld_c, 32)
            pe.wait_ge(silu_done, 1)
            for n, k in enumerate((0, 1, 2, 5)):
                mm = pe.matmul(psum[:, 0, 2 * n:2 * n + 2], wmod_sb[:, k * C:(k + 1) * C], silu_c[:, :],
                               start=True, stop=True)
            mm.then_inc(mod_mm, 1)
            pe.wait_ge(ident_ready, 3)
            turn(0)
            pe.wait_ge(ld_w, 128)
            pe.wait_ge(w_turned, 1)
            project_cols(0, K_BANKS, w_dh[:, 1, :], k_mm)
            pe.wait_ge(mod_cols_done, 3)
            project_cols(0, Q_BANKS, w_dh[:, 0, :], q_mm)
            turn(1)
            project_cols(0, PRE_BANKS, weights[:, 3, :], pre_mm, ((hT_done[0], 1), (hT_done[0], 2)))
            project_values(0, hT_done[1])
            project_cols(1, K_BANKS, w_dh[:, 1, :], k_mm, ((k_out[0], 1), (pre_out[0], 1)))
            project_cols(1, Q_BANKS, w_dh[:, 0, :], q_mm, ((q_out[0], 1), (q_out[0], 2)))
            pe.wait_ge(k_out[0], 2)
            for j in range(4):
                pe_logits(pe, (0, 0, 0), j)
            project_values(1, k_out[1])
            project_cols(1, PRE_BANKS, weights[:, 3, :], pre_mm, ((q_out[1], 1), (q_out[1], 2)))
            pe.wait_ge(k_loaded[0], 96)
            pe.wait_ge(pre_out[0], 2)
            pe.wait_ge(v_out[0], 2)
            for h in range(LEAD):
                for c in range(4):
                    pe_score_chunk(pe, (0, 0, 0), h, c, first=True)
                if h == LEAD - 3:
                    pe.wait_ge(l_evac, 4)
                    for j in range(4):
                        pe_logits(pe, (1, 1, 0), j)
            pe.wait_ge(l_evac, 8)
            pe_max_rows(pe, (0, 0, 0), 0)
            pe.wait_ge(minus_k_loaded[0], 96)
            pe.wait_ge(consts, 7)
            pe.wait_ge(pre_out[1], 2)
            pe.wait_ge(v_out[1], 2)
            pe_block(pe, (0, 0, 0), first=True)
            pe.wait_ge(minus_k_loaded[1], 96)
            pe.wait_ge(consts, 12)
            with pe.Fori(0, LOOPS) as k:
                pe_block(pe, (k * 2 + 1, 1, k))
                pe_block(pe, (k * 2 + 2, 0, k + 1))
            pe_block(pe, (BLOCKS - 1, 1, NT // 2 - 1), last=True)
            turn_weights(pe)
            pe.wait_ge(exp_done, BLOCKS * STEPS)
            pe.wait_ge(av_evac, BLOCKS * GROUPS - 1)
            for m in range(NT):
                mm = pe_values(pe, 1, GROUPS - 1, m)
            mm.then_inc(av_done, 1)
            pe.wait_ge(av_evac, BLOCKS * GROUPS)
            for k in range(2):
                pe.wait_ge(norm_done, 2 * BLOCKS - 2 + k)
                pe_norm(pe, k)
            ffn_pe(pe)

        @block.scalar
        def _(act):
            act.dma_start(silu_in[:, :], cond.rearrange("b c -> c b"), allow_slow_non_contiguous=True).then_inc(ld_c, 16)
            act.dma_start(wmod_sb, wmod).then_inc(ld_c, 16)
            for n, w in enumerate((wq, wk, wv, wpre, wproj)):
                act.dma_start(weights[:, n, :], w).then_inc(ld_w, 16)
            act.dma_start(small[:, 1:2], bpre.rearrange("(c o) -> c o", o=1)).then_inc(ld_w, 16)
            act.dma_start(small[:, 3:4], bproj.rearrange("(c o) -> c o", o=1)).then_inc(ld_w, 16)
            act.dma_start(small[:, 2:3], pi.partition_broadcast(P)).then_inc(ld_w, 16)
            act.wait_ge(ld_c, 32)
            act.activation(silu_c[:, :], silu_in[:, :], ACT.Silu).then_inc(silu_done, 1)
            act.wait_ge(consts, 1)
            for b in range(BATCH):
                act.wait_ge(bn_done[b], NT)
                act.activation(std[:, b * NT:(b + 1) * NT], mv[:, b * NT:(b + 1) * NT, 1], ACT.Sqrt,
                               bias=small[:, 0:1]).then_inc(std_done[b], 1)

            def columns(b):
                for half, bank in enumerate(TURN_BANKS[b]):
                    act.wait_ge(turned[b], half + 1)
                    act.activation(hT[:, b, half * CH:(half + 1) * CH], psum[:, bank, :], ACT.Identity,
                                   bias=mod_cols[:, 0, b:b + 1], scale=mod_cols[:, 1, b:b + 1]).then_inc(hT_done[b], 1)

            def queries_out(b):
                for half in range(2):
                    if b:
                        act.wait_ge(q_split[0], 4)
                    act.wait_ge(q_mm[b], half + 1)
                    act.activation(qk32[:, 0, half * CH:(half + 1) * CH], psum[:, Q_BANKS[b][half], :], ACT.Copy,
                                   scale=float(DH) ** -0.5).then_inc(q_out[b], 1)

            def pre_columns(b):
                for half in range(2):
                    act.wait_ge(pre_mm[b], half + 1)
                    act.activation(preT[:, b, half * CH:(half + 1) * CH], psum[:, PRE_BANKS[b][half], :], ACT.Silu,
                                   bias=small[:, 1:2]).then_inc(pre_out[b], 1)
                act.wait_ge(pi_scaled, 1)
                act.wait_ge(pre_out[b], 2)
                act.activation(pre_blk[:, b, :], preT[:, b, 0:QB], ACT.Copy, scale=small[:, 4:5]).then_inc(pre_first[b], 1)
                if b:
                    act.wait_ge(pre_stored[0], 16)
                act.activation(preS, preT[:, b, :], ACT.Copy, scale=small[:, 4:5]).then_inc(pre_scaled[b], 1)

            act.wait_ge(mod_cols_done, 3)
            act.wait_ge(ld_w, 128)
            columns(0)
            queries_out(0)
            split_part(act, 0, 0, 0)
            columns(1)
            pre_columns(0)
            split_part(act, 0, 0, 1)
            for half in range(2):
                act.wait_ge(k_split[0], 4)
                act.wait_ge(k_mm[1], half + 1)
                act.activation(qk32[:, 1, half * CH:(half + 1) * CH], psum[:, K_BANKS[1][half], :],
                               ACT.Copy).then_inc(k_out[1], 1)
            for j in range(4):
                act_logits(act, (0, 0, 0), j)
            split_part(act, 1, 1, 0)
            queries_out(1)
            split_part(act, 1, 0, 0)
            for half in range(2):
                act.wait_ge(v_mm[1], half + 1)
                act.wait_ge(consts, 5)
                act.activation(v_aug[:, 1, 4 * half:4 * half + 4, :, 0:DH],
                               psum[:, V_BANKS[1][half], :].rearrange("p (t h d) -> p t h d", t=4, d=DH),
                               ACT.Copy).then_inc(v_out[1], 1)
            pre_columns(1)
            split_part(act, 1, 1, 1)
            split_part(act, 1, 0, 1)
            act.wait_ge(q_stored[1], 48)
            for j in range(4):
                act_logits(act, (1, 1, 0), j)
            act_max_rows(act, (0, 0, 0), 0, first=True)
            for b in range(BATCH):
                act.wait_ge(q_stored[b], 48)
                act.wait_ge(k_loaded[b], 96)
                act.wait_ge(minus_k_loaded[b], 96)
                act.wait_ge(pre_stored[b], 16)
                act.wait_ge(h_stored[b], 16)
                act.wait_ge(v_mm[b], 2)
            act_block(act, (0, 0, 0), first=True)
            with act.Fori(0, LOOPS) as k:
                act_block(act, (k * 2 + 1, 1, k))
                act_block(act, (k * 2 + 2, 0, k + 1))
            act_block(act, (BLOCKS - 1, 1, NT // 2 - 1), last=True)
            act_values(act, (BLOCKS, 0, 0), GROUPS - 1, BLOCKS * GROUPS)
            ffn_act(act)

        @block.vector
        def _(dve):
            dve.memset(kd[32:64, 0, :, :].bitcast(F32), ONE_PAIR).then_inc(k_ones, 1)

            def moments(b):
                dve.wait_ge(x_loaded[b], 16)
                for k in range(NT):
                    dve.bn_stats(stats[:, b * NT + k, :], xs[:, b * NT + k, :]).then_inc(bn_stats_done[b], 1)
                for k in range(NT):
                    dve.wait_ge(bn_stats_done[b], k + 1)
                    dve.bn_aggr(mv[:, b * NT + k, :], stats[:, b * NT + k, :]).then_inc(bn_done[b], 1)

            def normed(b):
                cols = slice(b * NT, (b + 1) * NT)
                dve.wait_ge(std_done[b], 1)
                dve.reciprocal(rstd[:, cols], std[:, cols]).then_inc(rstd_done[b], 1)
                dve.wait_ge(rstd_done[b], 1)
                for k in range(NT):
                    t = b * NT + k
                    dve.tensor_scalar(xhat[:, t, :], xs[:, t, :], mv[:, t, 0:1], rstd[:, t:t + 1], ALU.subtract,
                                      ALU.mult).then_inc(xhat_done[b], 1)

            moments(0)
            dve.wait_ge(mod_mm, 1)
            dve.tensor_copy(mod_cols[:, 0, :], psum[:, 0, 0:2]).then_inc(mod_cols_done, 1)
            dve.tensor_scalar(mod_cols[:, 1, :], psum[:, 0, 2:4], 1.0, None, ALU.add).then_inc(mod_cols_done, 1)
            normed(0)
            dve.tensor_scalar(gate_cols[:, 0, :], psum[:, 0, 4:8], 0.0, 2.0, ALU.is_ge, ALU.mult).then_inc(gate_steps, 1)
            dve.wait_ge(gate_steps, 1)
            dve.tensor_scalar(gate_cols[:, 1, :], gate_cols[:, 0, :], -1.0, None, ALU.add).then_inc(gate_steps, 1)
            dve.scalar_tensor_tensor(out=gate_cols[:, 2, :], in0=gate_cols[:, 0, :], scalar=-1.0, in1=psum[:, 0, 4:8],
                                     op0=ALU.add, op1=ALU.mult).then_inc(gate_steps, 1)
            dve.wait_ge(gate_steps, 3)
            dve.scalar_tensor_tensor(out=mod_cols[:, 2:4, :].rearrange("p k b -> p (k b)"), in0=gate_cols[:, 2, :],
                                     scalar=0.25, in1=gate_cols[:, 1, :], op0=ALU.max,
                                     op1=ALU.mult).then_inc(mod_cols_done, 1)
            moments(1)
            normed(1)
            dve.wait_ge(ld_w, 128)
            dve.tensor_scalar(small[:, 4:5], small[:, 2:3], float(C) ** -0.5, None, ALU.mult).then_inc(pi_scaled, 1)
            for half in range(2):
                dve.wait_ge(k_mm[0], half + 1)
                dve.tensor_copy(qk32[:, 1, half * CH:(half + 1) * CH], psum[:, K_BANKS[0][half], :]).then_inc(k_out[0], 1)
            split_part(dve, 0, 1, 0)
            split_rest(dve, 0, 1, 0)
            split_part(dve, 0, 1, 1)
            split_rest(dve, 0, 1, 1)
            split_rest(dve, 0, 0, 0)
            dve.wait_ge(consts, 5)
            for half in range(2):
                dve.wait_ge(v_mm[0], half + 1)
                dve.tensor_copy(v_aug[:, 0, 4 * half:4 * half + 4, :, 0:DH],
                                psum[:, V_BANKS[0][half], :].rearrange("p (t h d) -> p t h d", t=4, d=DH)
                                ).then_inc(v_out[0], 1)
            split_rest(dve, 0, 0, 1)
            dve.wait_ge(k_split[0], 4)
            dve.tensor_scalar(parts[0][2], parts[0][1], -1.0, None, ALU.mult).then_inc(k_negated[0], 1)
            dve.wait_ge(v_out[0], 2)
            dve.memset(psum[:, AVB, :], 0.0).then_inc(av_zeroed, 1)
            dve.wait_ge(store_pad, 64)
            for h in range(LEAD):
                for c in range(4):
                    dve_max_chunk(dve, (0, 0, 0), h, c)
                if h % 8 == 7:
                    dve_max_parts(dve, (0, 0, 0), h // 8, first=True)
            dve_block(dve, (0, 0, 0), first=True)
            chunk = dve.alloc_register("next_score_chunk")
            dve.reg_mov(chunk, CHUNKS + 4 * LEAD + 1)
            with dve.Fori(0, LOOPS) as k:
                dve_block(dve, (k * 2 + 1, 1, k), chunk)
                dve_block(dve, (k * 2 + 2, 0, k + 1), chunk)
            dve_block(dve, (BLOCKS - 1, 1, NT // 2 - 1), last=True)
            copy_weights(dve)
            for k in range(2):
                dve_norm(dve, (BLOCKS - 1, 1, NT // 2 - 1), k)
            ffn_dve(dve)


_INPUTS = ("L0_attn_x", "L0_attn_Wq", "L0_attn_Wk", "L0_attn_Wv", "L0_attn_Wproj", "L0_attn_bproj",
           "L0_attn_Wpre", "L0_attn_bpre", "L0_attn_pi", "L0_c", "L0_wmod", "L0_ffn_router_w",
           "L0_ffn_gate_up_proj", "L0_ffn_down_proj", "L0_ffn_shared_gate_w", "L0_ffn_shared_up_w",
           "L0_ffn_shared_down_w")


def kernel(**inputs):
    import concourse.bacc as bacc
    from concourse.bass_utils import run_bass_kernel_spmd

    nc = bacc.Bacc("TRN2", target_bir_lowering=False, num_devices=1)
    arrays, args = {}, []
    for name in _INPUTS:
        a = np.ascontiguousarray(inputs[name])
        arrays[name] = a
        args.append(nc.dram_tensor(name, a.shape, mybir.dt.from_np(a.dtype), kind="ExternalInput").ap())
    shape = arrays["L0_attn_x"].shape
    args.append(nc.dram_tensor("out", shape, F32, kind="ExternalOutput").ap())
    build(nc, *args)
    return run_bass_kernel_spmd(nc, [arrays], core_ids=[0]).results[0]["out"]
```
